# Optimizing a Trainium2 kernel written in Bass

```python
import numpy as np
import jax
import jax.numpy as jnp

def _softmax(x, axis=-1):
    return jax.nn.softmax(x, axis=axis)

def _gelu(x):
    return jax.nn.gelu(x, approximate=True)

def _silu(x):
    return jax.nn.silu(x)

def _sigmoid(x):
    return jax.nn.sigmoid(x)

def _layernorm(x, axis=-1, eps=1e-05):
    m = jnp.mean(x, axis=axis, keepdims=True)
    v = jnp.var(x, axis=axis, keepdims=True)
    return (x - m) / jnp.sqrt(v + eps)

def _scatter_add(tgt, idx, src, axis=0):
    return tgt.at[idx].add(src)

def _segment_sum(src, seg, n):
    return jax.ops.segment_sum(src, seg, n)
kernel_name = 'mk_conv_preact_d2_conv_nhwc256_r2_291665'

def setup_inputs(seed: int=0):
    np.random.seed(seed)
    _w = jnp.asarray

    def _rec_inputs():
        import jax
        import jax.numpy as jnp
        _gk = jax.random.key(seed)
        x = 7.22e-05 + 1 * jax.random.normal(jax.random.fold_in(_gk, 1), (32, 32, 32, 128), jnp.float32)
        return x
    x = _rec_inputs()

    def _L0_conv_setup():
        import jax, jax.numpy as jnp
        import numpy as np
        B, V, H, CIN, S = (32, 32, 32, 128, 128)
        key = jax.random.key(seed)
        k1, k2 = jax.random.split(key)
        x = jax.random.normal(k1, (B, V, H, CIN), dtype=jnp.float32)
        accumulators = jax.random.uniform(k2, (V, H, CIN, S), dtype=jnp.float32, minval=0.1, maxval=1.1)
        return {'x': x, 'accumulators': accumulators}
    _L0_conv_all = _L0_conv_setup()
    _L0_conv_in = {k: v for k, v in _L0_conv_all.items() if k in ('accumulators',)}
    del _L0_conv_all

    def _L1_conv_setup():
        import jax, jax.numpy as jnp
        import numpy as np
        NEG_SLOPE = 0.01
        LN_EPS = 1e-05
        L2_EPS = 1e-12
        key = jax.random.key(seed)
        ks = jax.random.split(key, 8)
        B, T, N, C = (16, 32, 32, 128)
        local_feat = jax.random.normal(ks[0], (B, T, N, C), dtype=jnp.float32)
        global_feat = jax.random.normal(ks[1], (B, C), dtype=jnp.float32)
        pos = jax.random.normal(ks[2], (B, T * N, 3), dtype=jnp.float32)
        adj_w = jax.random.normal(ks[3], (C, C), dtype=jnp.float32) * (1.0 / np.sqrt(C))
        affine_w = jax.random.normal(ks[4], (C, C), dtype=jnp.float32) * np.sqrt(2.0 / C)
        affine_b = jnp.zeros((C,), dtype=jnp.float32)
        ln_g = jnp.ones((C,), dtype=jnp.float32)
        ln_b = jnp.zeros((C,), dtype=jnp.float32)
        return {'local_feat': local_feat, 'global_feat': global_feat, 'pos': pos, 'adj_w': adj_w, 'affine_w': affine_w, 'affine_b': affine_b, 'ln_g': ln_g, 'ln_b': ln_b}
    _L1_conv_all = _L1_conv_setup()
    _L1_conv_in = {k: v for k, v in _L1_conv_all.items() if k in ('global_feat', 'pos', 'adj_w', 'affine_w', 'affine_b', 'ln_g', 'ln_b')}
    del _L1_conv_all
    return {'x': x, 'L0_conv_accumulators': _L0_conv_in['accumulators'], 'L1_conv_global_feat': _L1_conv_in['global_feat'], 'L1_conv_pos': _L1_conv_in['pos'], 'L1_conv_adj_w': _L1_conv_in['adj_w'], 'L1_conv_affine_w': _L1_conv_in['affine_w'], 'L1_conv_affine_b': _L1_conv_in['affine_b'], 'L1_conv_ln_g': _L1_conv_in['ln_g'], 'L1_conv_ln_b': _L1_conv_in['ln_b']}

def reference(x, L0_conv_accumulators, L1_conv_global_feat, L1_conv_pos, L1_conv_adj_w, L1_conv_affine_w, L1_conv_affine_b, L1_conv_ln_g, L1_conv_ln_b):
    import jax
    import jax.numpy as jnp

    def _L0_conv_ref(x, accumulators):
        import jax, jax.numpy as jnp
        import numpy as np
        B, V, H, CIN, S = (32, 32, 32, 128, 128)
        log_w = jax.nn.log_softmax(jnp.log(accumulators), axis=2)
        xs = jnp.transpose(x, (1, 2, 0, 3))
        x_max = jnp.max(xs, axis=-1, keepdims=True)
        w_max = jnp.max(log_w, axis=2, keepdims=True)
        prod = jnp.einsum('vhbk,vhks->vhbs', jnp.exp(xs - x_max), jnp.exp(log_w - w_max))
        out_scopes_first = jnp.log(prod) + x_max + w_max
        return jnp.transpose(out_scopes_first, (2, 0, 1, 3))

    def _L1_conv_ref(local_feat, global_feat, pos, adj_w, affine_w, affine_b, ln_g, ln_b):
        import jax, jax.numpy as jnp
        import numpy as np
        NEG_SLOPE = 0.01
        LN_EPS = 1e-05
        L2_EPS = 1e-12
        B, T, N, C = local_feat.shape
        x = local_feat.reshape(B, T * N, C)
        nrm = jnp.sqrt(jnp.sum(x * x, axis=-1, keepdims=True))
        nf = x / jnp.maximum(nrm, L2_EPS)
        A = jnp.einsum('bnc,cd,bmd->bnm', nf, adj_w, nf)
        A = 5.0 * (A - jnp.max(A, axis=-1, keepdims=True))
        A = jax.nn.softmax(A, axis=-1)
        h = jnp.einsum('bmc,dc->bmd', x, affine_w) + affine_b
        h = jnp.einsum('bnm,bmc->bnc', A, h)
        mu = jnp.mean(h, axis=-1, keepdims=True)
        var = jnp.mean(jnp.square(h - mu), axis=-1, keepdims=True)
        h = (h - mu) / jnp.sqrt(var + LN_EPS) * ln_g + ln_b
        h = jnp.where(h >= 0, h, NEG_SLOPE * h)
        return h.reshape(B, T, N, C)

    def _gn(v, G=32, eps=1e-05):
        B_, H_, W_, C_ = v.shape
        g = v.reshape(B_, H_, W_, G, C_ // G)
        m = jnp.mean(g, axis=(1, 2, 4), keepdims=True)
        s = jnp.var(g, axis=(1, 2, 4), keepdims=True)
        return ((g - m) / jnp.sqrt(s + eps)).reshape(v.shape)

    def _ln_c(v, eps=1e-06):
        m = jnp.mean(v, axis=-1, keepdims=True)
        s = jnp.var(v, axis=-1, keepdims=True)
        return (v - m) / jnp.sqrt(s + eps)

    def _ln_t(v, eps=1e-05):
        m = jnp.mean(v, axis=-1, keepdims=True)
        s = jnp.var(v, axis=-1, keepdims=True)
        return (v - m) / jnp.sqrt(s + eps)

    def _to_tokens(v):
        B_, H_, W_, C_ = v.shape
        return v.reshape(B_, H_ * W_, C_)

    def _from_tokens(t, like):
        return t.reshape(like.shape)
    x = x + _L0_conv_ref(_gn(x), L0_conv_accumulators)
    x = x + _L1_conv_ref(_gn(x), L1_conv_global_feat, L1_conv_pos, L1_conv_adj_w, L1_conv_affine_w, L1_conv_affine_b, L1_conv_ln_g, L1_conv_ln_b)
    return x

_drawn_inputs = setup_inputs


def setup_inputs(seed=0):
    import zlib

    import numpy as np

    out = dict(_drawn_inputs(seed))
    spreads = {'L1_conv_affine_b': (0.0, 0.1), 'L1_conv_ln_g': (1.0, 0.2), 'L1_conv_ln_b': (0.0, 0.1)}
    factors = {}
    for name, (base, spread) in spreads.items():
        noise = np.random.default_rng([zlib.crc32(name.encode()), seed]).standard_normal(out[name].shape)
        drawn = base * np.exp(spread * noise) if base else spread * noise
        out[name] = jnp.asarray(drawn.astype(out[name].dtype))
    for name, factor in factors.items():
        out[name] = (out[name] * factor).astype(out[name].dtype)
    return out
```

```python
from contextlib import ExitStack

import concourse.bass as bass
import numpy as np
from concourse import mybir

F32 = mybir.dt.float32
F32R = mybir.dt.float32r
I32 = mybir.dt.int32
ALU = mybir.AluOpType
ACT = mybir.ActivationFunctionType
AX = mybir.AxisListType

P = 128
B = 32
NPOS = 1024
C = 128
G = 32
GC = C // G
Q = P // B
J = NPOS // Q
GN_EPS, LN_EPS, NORM_MIN, SLOPE, SHARP = 1e-5, 1e-5, 1e-12, 0.01, 5.0

CJ = 4
CW = CJ * C
NCH = J // CJ
WS = 4
ZS = 4
U0 = 8
SP0 = 4
SP1 = NCH // U0
GPC = G // U0

TT = NPOS // P
HT = TT // 2
HW = HT * C
UN = 2 * TT
SB = 4
PB = 2
LAG = 2
LIMIT = 64.0


def build(nc, x, acc, adj_w, aff_w, aff_b, ln_g, ln_b, stat_dram, out):
    ctx = ExitStack()
    with ctx:
        def sem(name):
            return ctx.enter_context(nc.semaphore(name))

        def sb(name, shape, dt=F32, c=ctx):
            return c.enter_context(nc.sbuf_tensor(name, shape, dt))

        X = sb("X", [P, J, C])
        ident = sb("ident", [P, P])
        Ac = sb("Ac", [P, C])
        b1 = sb("b1", [P, C])
        gB = sb("gB", [P, C])
        lbB = sb("lbB", [P, C])
        Whi = sb("Whi", [P, C], F32R)
        Wlo = sb("Wlo", [P, C], F32R)
        half_p = sb("half_p", [P, TT])
        half_n = sb("half_n", [P, G])
        MR = sb("MR", [P, 2, G])
        flag = sb("flag", [1, 1], I32)

        l0 = ExitStack()
        Wt = sb("Wt", [P, WS, Q, CJ, C], c=l0)
        Z = sb("Z", [P, ZS, CJ, C], c=l0)
        E = sb("E", [P, 2, CJ, C], c=l0)
        ET = sb("ET", [P, 2, CJ, C], c=l0)
        LP = sb("LP", [P, 2, CJ, C], c=l0)
        LS = sb("LS", [P, 2, CJ, C], c=l0)
        nmx = sb("nmx", [P, ZS, CJ], c=l0)
        st = sb("st", [P, SP1, G, 6], c=l0)
        dev = sb("dev", [P, G, SP1, 2], c=l0)
        gsum = sb("gsum", [P, G], c=l0)
        gvar = sb("gvar", [P, G], c=l0)
        col = sb("col", [P, 1], c=l0)
        mcol = sb("mcol", [P, 2], c=l0)
        ones = sb("ones", [P, B], c=l0)
        same_image = sb("same_image", [P, P], c=l0)
        adj_sb = sb("adj_sb", [P, C], c=l0)
        aff_sb = sb("aff_sb", [P, C], c=l0)
        l0.close()
        l1 = ExitStack()
        nTh = sb("nTh", [P, 2, NPOS], F32R, l1)
        nTl = sb("nTl", [P, 2, NPOS], F32R, l1)
        uTh = sb("uTh", [P, 2, NPOS], F32R, l1)
        uTl = sb("uTl", [P, 2, NPOS], F32R, l1)
        hh = sb("hh", [P, 2, TT, C], F32R, l1)
        hl = sb("hl", [P, 2, TT, C], F32R, l1)
        Ph = sb("Ph", [P, PB, HW], F32R, l1)
        Pl = sb("Pl", [P, PB, HW], F32R, l1)
        tok = sb("tok", [P, TT, C], c=l1)
        nT = sb("nT", [P, NPOS], c=l1)
        OT = sb("OT", [P, HW], c=l1)
        Y = sb("Y", [P, 2, HT, C], c=l1)
        YQ = sb("YQ", [P, HT, C], c=l1)
        res = sb("res", [P, HT, C], c=l1)
        mrb = sb("mrb", [P, 2, G], c=l1)
        n2 = sb("n2", [P, TT], c=l1)
        nrm = sb("nrm", [P, TT], c=l1)
        rn = sb("rn", [P, TT], c=l1)
        lastc = sb("lastc", [P, HT], c=l1)
        rs = sb("rs", [P, HT], c=l1)
        vs = sb("vs", [P, HT], c=l1)
        fac = sb("fac", [P, HT], c=l1)
        den = sb("den", [P, HT], c=l1)
        gmx = sb("gmx", [P, 1], c=l1)
        gnm = sb("gnm", [P, 1], c=l1)
        l1.close()

        PS = ctx.enter_context(nc.psum_tensor("PS", [P, 8, 512], F32))
        TP = [PS[:, i, :] for i in (0, 1)]
        PP = [PS[:, i, :] for i in (2, 3)]
        SS = [PS[:, i, :] for i in (4, 5)]
        MISC = PS[:, 6, :]
        SL = [PS[:, i, :] for i in range(SB)]
        OO = [PS[:, i, :] for i in (4, 5)]
        WB = [PS[:, i, :] for i in (6, 7)]
        EB = [WB[1], WB[0]]

        s_par = sem("s_par")
        s_const = sem("s_const")
        s_wsplit = sem("s_wsplit")
        s_afft = sem("s_afft")
        s_ac = sem("s_ac")
        s_sq = sem("s_sq")
        s_norm = sem("s_norm")
        s_flag = sem("s_flag")
        s_x = [sem(f"s_load{i}") for i in range(SP0)]
        s_w = [sem(f"s_weights{i}") for i in range(WS)]
        s_bn = sem("s_bn")
        s_st = sem("s_st")
        s_gs = sem("s_gs")
        s_gp = sem("s_gp")
        s_zc = sem("s_zc")
        s_z = sem("s_z")
        s_min = sem("s_min")
        s_e = sem("s_e")
        s_tr = sem("s_tr")
        s_et = sem("s_et")
        s_prod = sem("s_prod")
        s_ln = sem("s_ln")
        s_lw = sem("s_lw")
        s_x1 = sem("s_x1")
        s_stout = sem("s_stout")
        s_mrb = sem("s_mrb")
        s_tok = sem("s_tok")
        s_free = sem("s_free")
        s_res = sem("s_res")
        s_out = [sem(f"s_out{i}") for i in (0, 1)]
        s_cent = sem("s_cent")
        s_gn = sem("s_gn")
        s_sqr = sem("s_sqr")
        s_n2 = sem("s_n2")
        s_root = sem("s_root")
        s_nmax = sem("s_nmax")
        s_rn = sem("s_rn")
        s_unit = sem("s_unit")
        s_T = sem("s_T")
        s_nTh = sem("s_nTh")
        s_nT = sem("s_nT")
        s_nTl = sem("s_nTl")
        s_U = sem("s_U")
        s_uTh = sem("s_uTh")
        s_uTl = sem("s_uTl")
        s_H = sem("s_H")
        s_h = sem("s_h")
        s_hh = sem("s_hh")
        s_hl = sem("s_hl")
        s_log = sem("s_log")
        s_exp = sem("s_exp")
        s_ph = sem("s_ph")
        s_pl = sem("s_pl")
        s_av = sem("s_av")
        s_ot = sem("s_ot")
        s_E = sem("s_E")
        s_y = sem("s_y")
        s_sum = sem("s_sum")
        s_den = sem("s_den")
        s_last = sem("s_last")
        s_yq = sem("s_yq")
        s_v = sem("s_v")
        s_isd = sem("s_isd")
        s_fac = sem("s_fac")
        s_y1 = sem("s_y1")
        s_y2 = sem("s_y2")
        s_y3 = sem("s_y3")
        s_y4 = sem("s_y4")
        g_log = sem("g_log")
        g_max = sem("g_max")
        g_neg = sem("g_neg")
        g_exp = sem("g_exp")
        g_tr = sem("g_tr")
        g_cp = sem("g_cp")
        g_av = sem("g_av")

        NST = 8
        NV = 5
        NCONST = 5 + 1 + 2 * Q - 1
        block = ctx.enter_context(nc.Block())
        out_v = out.rearrange("b (p t) c -> b p t c", t=TT)

        @block.sync
        def _(sp):
            xj = J // SP0
            for i in range(SP0):
                sp.dma_start(X[:, i * xj:(i + 1) * xj, :], x[:, i * xj * C:(i + 1) * xj * C]
                             .rearrange("p (j c) -> p j c", c=C)).then_inc(s_x[i], 16)

            def load_weights(ch, slot, nth, wait):
                if wait:
                    sp.wait_ge(s_prod, nth)
                sp.dma_start(Wt[:, slot, :, :, :], acc[ch, :, :].rearrange(
                    "k (q i s) -> k q i s", q=Q, i=CJ)).then_inc(s_w[slot], 16)

            for ch in range(WS):
                load_weights(ch, ch, 0, False)
            with sp.Fori(1, NCH // WS) as r:
                for slot in range(WS):
                    load_weights(r * WS + slot, slot, r * WS + slot - WS + 1, True)

            sp.wait_ge(s_gp, 2)
            sp.dma_start(stat_dram, MR[0:B, :, :]).then_inc(s_stout, 16)
            sp.wait_ge(s_stout, 16)

            def gather(b):
                if b:
                    sp.wait_ge(s_free, b)
                sp.dma_start(mrb[:, :, :], stat_dram[b:b + 1, :, :].broadcast_to([P, 2, G])).then_inc(s_mrb, 16)
                for q in range(Q):
                    r = q * B + b
                    sp.dma_start(tok[q * B:(q + 1) * B, :, :],
                                 X[r:r + 1, :, :].rearrange("o (p t) c -> o p (t c)", t=TT)).then_inc(s_tok, 16)

            def gather_residual(b, e):
                if 2 * b + e:
                    sp.wait_ge(s_y4, 2 * b + e)
                for q in range(Q):
                    r = q * B + b
                    sp.dma_start(res[q * B:(q + 1) * B, :, :],
                                 X[r:r + 1, :, :].rearrange("o (p e t) c -> o p e (t c)", e=2, t=HT)[:, :, e, :])\
                        .then_inc(s_res, 16)

            def store(b, e):
                sp.wait_ge(s_y4, 2 * b + e + 1)
                sp.dma_start(out_v[b, :, e * HT:(e + 1) * HT, :], Y[:, e, :, :]).then_inc(s_out[e], 16)

            gather(0)
            gather_residual(0, 0)
            sp.wait_ge(s_flag, 1)
            bounded = sp.value_load(flag[0:1, 0:1], min_val=0, max_val=1)
            with sp.If(bounded == 1):
                for b in range(B):
                    if b + 1 < B:
                        gather(b + 1)
                    if b:
                        store(b - 1, 0)
                        gather_residual(b - 1, 1)
                        store(b - 1, 1)
                        gather_residual(b, 0)
                store(B - 1, 0)
                gather_residual(B - 1, 1)
                store(B - 1, 1)
            with sp.Else():
                for b in range(B):
                    store(b, 0)
                    gather_residual(b, 1)
                    store(b, 1)
                    if b + 1 < B:
                        gather(b + 1)
                        gather_residual(b + 1, 0)
            sp.wait_ge(s_out[0], 16 * B)
            sp.wait_ge(s_out[1], 16 * B)

        @block.gpsimd
        def _(pool):
            n = 0
            for t, v in ((ident, 0.0), (same_image, 0.0), (ones, 1.0), (half_p, 0.5), (half_n, -0.5)):
                pool.memset(t[:, :], v).then_inc(s_const, 1)
                n += 1
            for t, d in [(ident, 0)] + [(same_image, k * B) for k in range(1 - Q, Q)]:
                pool.wait_ge(s_const, n)
                pool.affine_select(out=t[:, :], in_=t[:, :], compare_op=ALU.not_equal, fill=1.0, base=-d,
                                   pattern=[[-1, P]], channel_multiplier=1).then_inc(s_const, 1)
                n += 1
            assert n == NCONST

            def inverse_deviation(turn):
                pool.wait_ge(s_st, NST * (turn + 1))
                pool.tensor_tensor(MR[:, 1, :], gvar[:, :], half_n[:, :], ALU.pow).then_inc(s_gp, 1)

            def normalise(c, u, first):
                xc = X[:, bass.ds(c * CJ, CJ), :].rearrange("p j (g k) -> p j g k", k=GC)
                z = Z[:, u % ZS, :, :].rearrange("p j (g k) -> p j g k", k=GC)
                if not first:
                    pool.wait_ge(s_e, c - ZS + 1)
                pool.tensor_tensor(z, MR[:, 0, :].unsqueeze(1).unsqueeze(3).broadcast_to([P, CJ, G, GC]), xc,
                                   ALU.subtract).then_inc(s_zc, 1)
                pool.wait_ge(s_zc, c + 1)
                pool.tensor_tensor(z, z, MR[:, 1, :].unsqueeze(1).unsqueeze(3).broadcast_to([P, CJ, G, GC]),
                                   ALU.mult).then_inc(s_z, 1)

            inverse_deviation(0)
            pool.wait_ge(s_gp, 1)
            for c in range(ZS):
                normalise(c, c, True)
            with pool.Fori(1, NCH // ZS) as i:
                for u in range(ZS):
                    normalise(i * ZS + u, u, False)
            inverse_deviation(1)

            def group_norm(b):
                t = tok[:, :, :].rearrange("p t (g k) -> p t g k", k=GC)
                pool.wait_ge(s_mrb, b * 16 + 16)
                pool.wait_ge(s_tok, b * (16 * Q) + 16 * Q)
                pool.tensor_tensor(t, t, mrb[:, 0, :].unsqueeze(1).unsqueeze(3).broadcast_to([P, TT, G, GC]),
                                   ALU.subtract).then_inc(s_cent, 1)
                pool.wait_ge(s_cent, b + 1)
                pool.tensor_tensor(t, t, mrb[:, 1, :].unsqueeze(1).unsqueeze(3).broadcast_to([P, TT, G, GC]),
                                   ALU.mult).then_inc(s_gn, 1)

            def root(b):
                pool.wait_ge(s_n2, b + 1)
                pool.tensor_tensor(nrm[:, :], n2[:, :], half_p[:, :], ALU.pow).then_inc(s_root, 1)

            def unit(b):
                pool.wait_ge(s_rn, b + 1)
                pool.tensor_tensor(tok[:, :, :], tok[:, :, :], rn[:, :].unsqueeze(2).broadcast_to([P, TT, C]),
                                   ALU.mult).then_inc(s_unit, 1)

            def squares(b, e):
                pool.wait_ge(s_last, b * 2 + (e + 1))
                pool.tensor_tensor(YQ[:, :, :], Y[:, e, :, :], Y[:, e, :, :], ALU.mult).then_inc(s_yq, 1)

            def inverse_sd(b, e):
                pool.wait_ge(s_v, (b * 2 + (e + 1)) * NV)
                pool.tensor_tensor(vs[:, :], vs[:, :], half_n[:, 0:HT], ALU.pow).then_inc(s_isd, 1)

            def add_beta(b, e):
                pool.wait_ge(s_y1, b * 2 + (e + 1))
                pool.tensor_tensor(Y[:, e, :, :], Y[:, e, :, :], lbB[:, :].unsqueeze(1).broadcast_to([P, HT, C]),
                                   ALU.add).then_inc(s_y2, 1)

            def add_residual(b, e):
                pool.wait_ge(s_y3, b * 2 + (e + 1))
                pool.wait_ge(s_res, (b * 2 + (e + 1)) * (16 * Q))
                pool.tensor_tensor(Y[:, e, :, :], Y[:, e, :, :], res[:, :, :], ALU.add).then_inc(s_y4, 1)

            def image(b, s, first=False, last=False):
                if not first:
                    squares(b - 1, 0)
                    inverse_sd(b - 1, 0)
                if not last:
                    group_norm(b + 1)
                if not first:
                    add_beta(b - 1, 0)
                    squares(b - 1, 1)
                if not last:
                    root(b + 1)
                    unit(b + 1)
                if not first:
                    add_residual(b - 1, 0)
                    inverse_sd(b - 1, 1)
                    add_beta(b - 1, 1)
                    add_residual(b - 1, 1)

            def attention():
                group_norm(0)
                root(0)
                unit(0)
                image(0, 0, first=True)
                image(1, 1)
                with pool.Fori(1, B // 2 - 1) as i:
                    image(i * 2, 0)
                    image(i * 2 + 1, 1)
                image(B - 2, 0)
                image(B - 1, 1, last=True)
                for e in (0, 1):
                    squares(B - 1, e)
                    inverse_sd(B - 1, e)
                    add_beta(B - 1, e)
                    add_residual(B - 1, e)

            def general():
                with pool.Fori(0, B) as b:
                    group_norm(b)
                    root(b)
                    unit(b)
                    for e in (0, 1):
                        squares(b, e)
                        inverse_sd(b, e)
                        add_beta(b, e)
                        add_residual(b, e)

            pool.wait_ge(s_flag, 1)
            bounded = pool.value_load(flag[0:1, 0:1], min_val=0, max_val=1)
            with pool.If(bounded == 1):
                attention()
            with pool.Else():
                general()

        @block.scalar
        def _(act):
            act.dma_start(adj_sb[:, :], adj_w).then_inc(s_par, 16)
            act.dma_start(aff_sb[:, :], aff_w).then_inc(s_par, 16)
            for t, v in ((b1, aff_b), (gB, ln_g), (lbB, ln_b)):
                act.dma_start(t[:, :], v.rearrange("(o c) -> o c", o=1).broadcast_to([P, C])).then_inc(s_par, 16)
            act.wait_ge(s_par, 16 * 5)
            act.activation(LP[:, 0, 0, :], adj_sb[:, :], ACT.Square, accum_out=col[:, :]).then_inc(s_sq, 1)

            def exps(c, u):
                act.wait_ge(s_min, c + 1)
                for i in range(CJ):
                    last = act.activation(E[:, u % 2, i, :], Z[:, u % ZS, i, :], ACT.Exp,
                                          bias=nmx[:, u % ZS, i:i + 1], scale=-1.0)
                last.then_inc(s_e, 1)

            def logs(c, u, early=False):
                act.wait_ge(s_prod, c + 1)
                if early:
                    act.wait_ge(s_sq, 1)
                else:
                    act.wait_ge(s_x1, c - 1)
                act.activation(LP[:, u % 2, :, :], PP[u % 2].rearrange("p (i c) -> p i c", c=C), ACT.Ln)
                act.activation(LS[:, u % 2, :, :], SS[u % 2].rearrange("p (i c) -> p i c", c=C), ACT.Ln)\
                    .then_inc(s_ln, 1)

            def step(c, u, first=False, last=False):
                if not last:
                    if not first:
                        act.wait_ge(s_tr, c)
                    exps(c + 1, u + 1)
                act.wait_ge(s_tr, c + 1)
                act.activation(ET[:, u % 2, :, :], TP[u % 2].rearrange("p (i c) -> p i c", c=C), ACT.Copy)\
                    .then_inc(s_et, 1)
                if not first:
                    logs(c - 1, u - 1, early=isinstance(c, int) and c <= 2)

            exps(0, 0)
            for c in range(U0):
                step(c, c, first=c == 0)
            with act.Fori(1, NCH // U0 - 1) as i:
                for u in range(U0):
                    step(i * U0 + u, U0 + u)
            for c in range(NCH - U0, NCH):
                step(c, c, last=c == NCH - 1)
            logs(NCH - 1, NCH - 1)

            def token_squares(b, first=False):
                act.wait_ge(s_gn, b + 1)
                if not first:
                    act.wait_ge(s_H, b * 2)
                act.activation(nT[:, :].rearrange("p (t c) -> p t c", c=C), tok[:, :, :], ACT.Square)\
                    .then_inc(s_sqr, 1)

            def tokens_T(b, s, e, freed):
                act.wait_ge(s_T, b * 2 + (e + 1))
                if freed is not None:
                    act.wait_ge(*freed)
                act.activation(nT[:, e * HW:(e + 1) * HW], WB[e], ACT.Copy).then_inc(s_nT, 1)
                act.activation(nTh[:, s, e * HW:(e + 1) * HW], WB[e], ACT.Copy).then_inc(s_nTh, 1)

            def queries_T(b, s, e):
                act.wait_ge(s_U, b * 2 + (e + 1))
                act.activation(uTh[:, s, e * HW:(e + 1) * HW], WB[e], ACT.Copy).then_inc(s_uTh, 1)

            def take_output(b, e, made, first=False):
                act.wait_ge(*made)
                if not first:
                    act.wait_ge(s_E, b * 2 + e)
                act.activation(OT[:, :], OO[e], ACT.Copy).then_inc(s_ot, 1)

            def take_rows(b, e, first=False):
                act.wait_ge(s_E, b * 2 + (e + 1))
                if not first:
                    act.wait_ge(s_out[e], b * 16)
                act.activation(Y[:, e, :, :], EB[e].rearrange("p (t c) -> p t c", c=C), ACT.Copy).then_inc(s_y, 1)

            def unit_step(b, k, first):
                sl = SL[k % SB]
                act.wait_ge(s_log, b * UN + (k + 1))
                act.activation(sl, sl, ACT.Exp, scale=SHARP).then_inc(s_exp, 1)
                act.wait_ge(s_exp, b * UN + (k + 1))
                if not (first and k < PB):
                    act.wait_ge(s_av, b * UN + (k + 1 - PB))
                act.activation(Ph[:, k % PB, :], sl, ACT.Copy).then_inc(s_ph, 1)

            def image(b, s, first=False, second=False, last=False):
                for k in range(UN):
                    unit_step(b, k, first)
                    if k == 0 and not first:
                        take_rows(b - 1, 0, first=second)
                    if k == 2 and not first:
                        take_output(b - 1, 1, (s_av, b * UN))
                    if k == 4 and not first:
                        take_rows(b - 1, 1, first=second)
                    if k == 6 and not last:
                        token_squares(b + 1)
                    if k == 9 and not last:
                        for e in (0, 1):
                            tokens_T(b + 1, 1 - s, e, None if first else (s_log, b * UN))
                    if k == 10:
                        take_output(b, 0, (s_av, b * UN + TT), first=first)
                    if k == 11 and not last:
                        for e in (0, 1):
                            queries_T(b + 1, 1 - s, e)

            def attention():
                token_squares(0, first=True)
                for e in (0, 1):
                    tokens_T(0, 0, e, (s_n2, 1))
                for e in (0, 1):
                    queries_T(0, 0, e)
                image(0, 0, first=True)
                image(1, 1, second=True)
                with act.Fori(1, B // 2 - 1) as i:
                    image(i * 2, 0)
                    image(i * 2 + 1, 1)
                image(B - 2, 0)
                image(B - 1, 1, last=True)
                take_rows(B - 1, 0)
                take_output(B - 1, 1, (s_av, B * UN))
                take_rows(B - 1, 1)

            def general():
                def general_image(b, first):
                    token_squares(b, first)
                    for e in (0, 1):
                        tokens_T(b, 0, e, (s_n2, b + 1))
                    for e in (0, 1):
                        queries_T(b, 0, e)
                    act.wait_ge(s_H, b * 2 + 2)
                    for t in range(TT):
                        act.wait_ge(g_neg, b * TT + (t + 1))
                        if t:
                            act.wait_ge(g_av, b * TT + t)
                        else:
                            act.wait_ge(s_hl, b * 2 + 2)
                        act.activation(tok[:, :, :].rearrange("p t c -> p (t c)"),
                                       PS[:, 0:2, :].rearrange("p a c -> p (a c)"), ACT.Exp,
                                       bias=gnm[:, :], scale=SHARP).then_inc(g_exp, 1)
                        for e in (0, 1):
                            act.wait_ge(g_tr, b * (2 * TT) + (2 * t + e + 1))
                            act.activation(nT[:, e * HW:(e + 1) * HW], SL[2 + e], ACT.Copy).then_inc(g_cp, 1)
                    for e in (0, 1):
                        take_output(b, e, (g_av, b * TT + (e + 1) * HT), first=first and e == 0)
                        take_rows(b, e, first=first)

                general_image(0, True)
                with act.Fori(1, B) as b:
                    general_image(b, False)

            act.wait_ge(s_flag, 1)
            bounded = act.value_load(flag[0:1, 0:1], min_val=0, max_val=1)
            with act.If(bounded == 1):
                attention()
            with act.Else():
                general()

        @block.vector
        def _(dve):
            dve.wait_ge(s_par, 16 * 5)
            dve.tensor_copy(Whi[:, :], adj_sb[:, :]).then_inc(s_wsplit, 1)
            dve.wait_ge(s_wsplit, 1)
            dve.tensor_tensor(Wlo[:, :], adj_sb[:, :], Whi[:, :].bitcast(F32), ALU.subtract).then_inc(s_wsplit, 1)
            dve.wait_ge(s_afft, 1)
            dve.reduce_sum(mcol[:, 0:1], PP[0][:, 0:C], AX.X).then_inc(s_ac, 1)
            dve.reduce_sum(mcol[:, 1:2], b1[:, :], AX.X).then_inc(s_ac, 1)
            dve.wait_ge(s_ac, 2)
            dve.tensor_scalar(mcol[:, :], mcol[:, :], 1.0 / C, None, ALU.mult).then_inc(s_ac, 1)
            dve.wait_ge(s_ac, 3)
            dve.tensor_scalar(Ac[:, :], PP[0][:, 0:C], mcol[:, 0:1], None, ALU.subtract).then_inc(s_ac, 1)
            dve.tensor_scalar(b1[:, :], b1[:, :], mcol[:, 1:2], None, ALU.subtract).then_inc(s_ac, 1)
            dve.wait_ge(s_ac, 5)
            dve.memset(Ac[:, C - 1:C], 0.0).then_inc(s_ac, 1)
            dve.memset(b1[:, C - 1:C], 1.0).then_inc(s_ac, 1)
            dve.wait_ge(s_norm, 1)
            dve.tensor_scalar(flag[0:1, 0:1], PP[1][0:1, 0:1], SHARP * SHARP, LIMIT * LIMIT, ALU.mult, ALU.is_le)\
                .then_inc(s_flag, 1)

            def piece_stats(m, pieces, groups):
                for g in groups:
                    last = dve.bn_stats(st[:, m, g, :] if isinstance(m, int) else st[:, bass.ds(m, 1), g, :],
                                        X[:, bass.ds(m * (J // pieces), J // pieces), g * GC:(g + 1) * GC])
                return last

            def statistics(turn, pieces):
                parts = st[:, 0:pieces, :, :].rearrange("p m g (e s) -> p g m e s", s=3)
                n = J // pieces * GC // 2
                d = dev[:, :, 0:pieces, :]
                at = NST * turn
                dve.wait_ge(s_bn, SP0 + SP1 * turn)
                dve.tensor_reduce(gsum[:, :], parts[:, :, :, :, 1], AX.XY, ALU.add).then_inc(s_st, 1)
                dve.wait_ge(s_gs, 2 * turn + 1)
                dve.tensor_scalar(MR[:, 0, :], MISC[:, 0:G], 1.0 / (2 * pieces * Q), None, ALU.mult).then_inc(s_st, 1)
                dve.wait_ge(s_st, at + 2)
                dve.tensor_tensor(d, parts[:, :, :, :, 1],
                                  MR[:, 0, :].unsqueeze(2).unsqueeze(3).broadcast_to([P, G, pieces, 2]),
                                  ALU.subtract).then_inc(s_st, 1)
                dve.wait_ge(s_st, at + 3)
                dve.tensor_tensor(d, d, d, ALU.mult).then_inc(s_st, 1)
                dve.wait_ge(s_st, at + 4)
                dve.tensor_reduce(gvar[:, :], d, AX.XY, ALU.add).then_inc(s_st, 1)
                dve.tensor_reduce(gsum[:, :], parts[:, :, :, :, 2], AX.XY, ALU.add).then_inc(s_st, 1)
                dve.wait_ge(s_st, at + 6)
                dve.scalar_tensor_tensor(out=gsum[:, :], in0=gvar[:, :], scalar=float(n), in1=gsum[:, :],
                                         op0=ALU.mult, op1=ALU.add).then_inc(s_st, 1)
                dve.wait_ge(s_gs, 2 * turn + 2)
                dve.tensor_scalar(gvar[:, :], MISC[:, G:2 * G], 1.0 / (NPOS * GC), GN_EPS, ALU.mult, ALU.add)\
                    .then_inc(s_st, 1)

            for m in range(SP0):
                dve.wait_ge(s_x[m], 16)
                piece_stats(m, SP0, range(G)).then_inc(s_bn, 1)
            statistics(0, SP0)

            def minima(c, u):
                dve.wait_ge(s_z, c + 1)
                dve.tensor_reduce(nmx[:, u % ZS, :], Z[:, u % ZS, :, :], AX.X, ALU.min).then_inc(s_min, 1)

            def result(c, u):
                dve.wait_ge(s_ln, c + 1)
                for i in range(CJ):
                    last = dve.scalar_tensor_tensor(out=LP[:, u % 2, i, :], in0=LP[:, u % 2, i, :],
                                                    scalar=nmx[:, u % ZS, i:i + 1], in1=LS[:, u % 2, i, :],
                                                    op0=ALU.subtract, op1=ALU.subtract)
                last.then_inc(s_lw, 1)
                dve.wait_ge(s_lw, c + 1)
                xc = X[:, bass.ds(c * CJ, CJ), :]
                dve.tensor_tensor(xc, LP[:, u % 2, :, :], xc, ALU.add).then_inc(s_x1, 1)

            minima(0, 0)
            minima(1, 1)

            def chunks(i, first=False, last=False):
                if not first:
                    dve.wait_ge(s_x1, i * U0)
                for u in range(U0):
                    if not (last and u + 2 >= U0):
                        minima(i * U0 + (u + 2), u + 2)
                    result(i * U0 + u, u)
                    if not first:
                        done = piece_stats(i - 1, SP1, range(u * GPC, (u + 1) * GPC))
                if not first:
                    done.then_inc(s_bn, 1)

            chunks(0, first=True)
            with dve.Fori(1, NCH // U0 - 1) as i:
                chunks(i)
            chunks(NCH // U0 - 1, last=True)
            dve.wait_ge(s_x1, NCH)
            piece_stats(SP1 - 1, SP1, range(G)).then_inc(s_bn, 1)
            statistics(1, SP1)

            def norms_squared(b):
                dve.wait_ge(s_sqr, b + 1)
                dve.reduce_sum(n2[:, :], nT[:, :].rearrange("p (t c) -> p t c", c=C), AX.X).then_inc(s_n2, 1)

            def inverse_norms(b):
                dve.wait_ge(s_root, b + 1)
                dve.tensor_scalar(nrm[:, :], nrm[:, :], NORM_MIN, None, ALU.max).then_inc(s_nmax, 1)
                dve.wait_ge(s_nmax, b + 1)
                dve.reciprocal(rn[:, :], nrm[:, :]).then_inc(s_rn, 1)

            def tokens_lower(b, s, e):
                dve.wait_ge(s_nTh, b * 2 + (e + 1))
                dve.tensor_tensor(nTl[:, s, e * HW:(e + 1) * HW], WB[e],
                                  nTh[:, s, e * HW:(e + 1) * HW].bitcast(F32), ALU.subtract).then_inc(s_nTl, 1)

            def queries_lower(b, s, e):
                dve.wait_ge(s_uTh, b * 2 + (e + 1))
                dve.tensor_tensor(uTl[:, s, e * HW:(e + 1) * HW], WB[e],
                                  uTh[:, s, e * HW:(e + 1) * HW].bitcast(F32), ALU.subtract).then_inc(s_uTl, 1)

            def values(b, e):
                dve.wait_ge(s_H, b * 2 + (e + 1))
                for t in range(HT):
                    last = dve.scalar_tensor_tensor(out=tok[:, e * HT + t, :], in0=WB[e][:, t * C:(t + 1) * C],
                                                    scalar=nrm[:, e * HT + t:e * HT + t + 1], in1=b1[:, :],
                                                    op0=ALU.mult, op1=ALU.add)
                last.then_inc(s_h, 1)

            def split_values(b, s, e, freed=None):
                if freed is not None:
                    dve.wait_ge(*freed)
                dve.wait_ge(s_h, b * 2 + (e + 1))
                dve.tensor_copy(hh[:, s, e * HT:(e + 1) * HT, :], tok[:, e * HT:(e + 1) * HT, :]).then_inc(s_hh, 1)
                dve.wait_ge(s_hh, b * 2 + (e + 1))
                dve.tensor_tensor(hl[:, s, e * HT:(e + 1) * HT, :], tok[:, e * HT:(e + 1) * HT, :],
                                  hh[:, s, e * HT:(e + 1) * HT, :].bitcast(F32), ALU.subtract).then_inc(s_hl, 1)

            def release(left):
                dve.wait_ge(*left)
                dve.memset(gmx[:, :], 0.0).then_inc(s_free, 1)

            def weights_lower(b, k):
                dve.wait_ge(s_ph, b * UN + (k + 1))
                dve.tensor_tensor(Pl[:, k % PB, :], SL[k % SB], Ph[:, k % PB, :].bitcast(F32), ALU.subtract)\
                    .then_inc(s_pl, 1)

            def last_channel(b, e):
                n = b * 2 + (e + 1)
                dve.wait_ge(s_y, n)
                dve.tensor_reduce(lastc[:, :], Y[:, e, :, 0:C - 1], AX.X, ALU.add).then_inc(s_sum, 1)
                dve.tensor_copy(den[:, :], Y[:, e, :, C - 1]).then_inc(s_den, 1)
                dve.wait_ge(s_sum, n)
                dve.wait_ge(s_den, n)
                dve.tensor_scalar(Y[:, e, :, C - 1], lastc[:, :], -1.0, None, ALU.mult).then_inc(s_last, 1)

            def variance(b, e):
                n = b * 2 + (e + 1)
                at = (b * 2 + e) * NV
                dve.reciprocal(rs[:, :], den[:, :]).then_inc(s_v, 1)
                dve.wait_ge(s_yq, n)
                dve.reduce_sum(vs[:, :], YQ[:, :, :], AX.X).then_inc(s_v, 1)
                dve.wait_ge(s_v, at + 2)
                dve.scalar_tensor_tensor(out=vs[:, :], in0=vs[:, :], scalar=1.0 / C, in1=rs[:, :],
                                         op0=ALU.mult, op1=ALU.mult).then_inc(s_v, 1)
                dve.wait_ge(s_v, at + 3)
                dve.tensor_tensor(vs[:, :], vs[:, :], rs[:, :], ALU.mult).then_inc(s_v, 1)
                dve.wait_ge(s_v, at + 4)
                dve.tensor_scalar(vs[:, :], vs[:, :], LN_EPS, None, ALU.add).then_inc(s_v, 1)

            def scale_rows(b, e):
                n = b * 2 + (e + 1)
                dve.wait_ge(s_isd, n)
                dve.tensor_tensor(fac[:, :], vs[:, :], rs[:, :], ALU.mult).then_inc(s_fac, 1)
                dve.wait_ge(s_fac, n)
                for t in range(HT):
                    last = dve.scalar_tensor_tensor(out=Y[:, e, t, :], in0=Y[:, e, t, :], scalar=fac[:, t:t + 1],
                                                    in1=gB[:, :], op0=ALU.mult, op1=ALU.mult)
                last.then_inc(s_y1, 1)

            def leaky(b, e):
                dve.wait_ge(s_y2, b * 2 + (e + 1))
                y = Y[:, e, :, :]
                dve.scalar_tensor_tensor(out=y, in0=y, scalar=SLOPE, in1=y, op0=ALU.mult, op1=ALU.max)\
                    .then_inc(s_y3, 1)

            def image(b, s, first=False, last=False):
                for k in range(UN):
                    weights_lower(b, k)
                    if k == 1 and not first:
                        last_channel(b - 1, 0)
                    if k == 2 and not first:
                        variance(b - 1, 0)
                    if k == 3 and not first:
                        scale_rows(b - 1, 0)
                    if k == 5 and not first:
                        last_channel(b - 1, 1)
                    if k == 6 and not first:
                        leaky(b - 1, 0)
                    if k == 7 and not last:
                        norms_squared(b + 1)
                        inverse_norms(b + 1)
                    if k == 8 and not first:
                        variance(b - 1, 1)
                    if k == 10:
                        if not last:
                            for e in (0, 1):
                                tokens_lower(b + 1, 1 - s, e)
                        if not first:
                            scale_rows(b - 1, 1)
                    if k == 12:
                        if not last:
                            for e in (0, 1):
                                queries_lower(b + 1, 1 - s, e)
                        if not first:
                            leaky(b - 1, 1)
                    if k == 13 and not last:
                        values(b + 1, 0)
                    if k == 14 and not last:
                        values(b + 1, 1)
                        split_values(b + 1, 1 - s, 0, None if first else (s_av, b * UN))
                    if k == 15 and not last:
                        split_values(b + 1, 1 - s, 1)
                        release((s_hl, b * 2 + 4))

            def prepare(b):
                norms_squared(b)
                inverse_norms(b)
                for e in (0, 1):
                    tokens_lower(b, 0, e)
                for e in (0, 1):
                    queries_lower(b, 0, e)
                for e in (0, 1):
                    values(b, e)
                for e in (0, 1):
                    split_values(b, 0, e)

            def finish(b, e):
                last_channel(b, e)
                variance(b, e)
                scale_rows(b, e)
                leaky(b, e)

            def attention():
                prepare(0)
                release((s_hl, 2))
                image(0, 0, first=True)
                image(1, 1)
                with dve.Fori(1, B // 2 - 1) as i:
                    image(i * 2, 0)
                    image(i * 2 + 1, 1)
                image(B - 2, 0)
                image(B - 1, 1, last=True)
                for e in (0, 1):
                    finish(B - 1, e)

            def general():
                with dve.Fori(0, B) as b:
                    prepare(b)
                    for t in range(TT):
                        n = b * TT + (t + 1)
                        dve.wait_ge(g_log, n)
                        dve.reduce_max(gmx[:, :], PS[:, 0:2, :].rearrange("p a c -> p (a c)"), AX.X).then_inc(g_max, 1)
                        dve.wait_ge(g_max, n)
                        dve.tensor_scalar(gnm[:, :], gmx[:, :], -SHARP, None, ALU.mult).then_inc(g_neg, 1)
                    release((g_av, b * TT + TT))
                    for e in (0, 1):
                        finish(b, e)

            dve.wait_ge(s_flag, 1)
            bounded = dve.value_load(flag[0:1, 0:1], min_val=0, max_val=1)
            with dve.If(bounded == 1):
                attention()
            with dve.Else():
                general()

        @block.tensor
        def _(pe):
            pe.wait_ge(s_const, NCONST)
            pe.wait_ge(s_par, 16 * 5)
            pe.transpose(PP[0][:, 0:C], aff_sb[:, :], ident[:, :]).then_inc(s_afft, 1)
            pe.wait_ge(s_sq, 1)
            pe.matmul(PP[1][0:B, 0:1], ones[:, :], col[:, :], start=True, stop=True).then_inc(s_norm, 1)

            def sum_quarters(turn):
                for h in (0, 1):
                    pe.wait_ge(s_st, NST * turn + (1, 7)[h])
                    pe.matmul(MISC[:, h * G:(h + 1) * G], same_image[:, :], gsum[:, :], start=True, stop=True)\
                        .then_inc(s_gs, 1)

            sum_quarters(0)

            def transposes(c, u, first=False):
                pe.wait_ge(s_e, c + 1)
                if not first:
                    pe.wait_ge(s_et, c - 1)
                for i in range(CJ):
                    last = pe.transpose(TP[u % 2][:, i * C:(i + 1) * C], E[:, u % 2, i, :], ident[:, :])
                last.then_inc(s_tr, 1)

            def products(c, u, nth, first=False):
                w = Wt[:, u % WS, :, :, :]
                pe.wait_ge(s_w[u % WS], nth)
                if not first:
                    pe.wait_ge(s_ln, c - 1)
                for q in range(Q):
                    pe.matmul(SS[u % 2][q * B:(q + 1) * B, :], ones[:, :], w[:, q, :, :].rearrange("k i s -> k (i s)"),
                              start=True, stop=True)
                pe.wait_ge(s_et, c + 1)
                for i in range(CJ):
                    for q in range(Q):
                        last = pe.matmul(PP[u % 2][q * B:(q + 1) * B, i * C:(i + 1) * C],
                                         ET[:, u % 2, i, q * B:(q + 1) * B], w[:, q, i, :], start=True, stop=True)
                last.then_inc(s_prod, 1)

            def chunks(i, first=False, last=False):
                for u in range(U0):
                    if not (last and u == U0 - 1):
                        transposes(i * U0 + (u + 1), u + 1, first=first and u == 0)
                    products(i * U0 + u, u, i * (U0 // WS * 16) + (u // WS + 1) * 16, first=first and u < 2)

            transposes(0, 0, first=True)
            chunks(0, first=True)
            with pe.Fori(1, NCH // U0 - 1) as i:
                chunks(i)
            chunks(NCH // U0 - 1, last=True)
            sum_quarters(1)

            def three(out_, lh, ll, rh, rl, start=True, stop=True):
                pe.matmul(out_, lh, rh, start=start, stop=False)
                pe.matmul(out_, lh, rl, start=False, stop=False)
                return pe.matmul(out_, ll, rh, start=False, stop=stop)

            def transpose_tokens(b, e, freed):
                pe.wait_ge(s_unit, b + 1)
                if freed is not None:
                    pe.wait_ge(*freed)
                for t in range(HT):
                    last = pe.transpose(WB[e][:, t * C:(t + 1) * C], tok[:, e * HT + t, :], ident[:, :])
                last.then_inc(s_T, 1)

            def queries(b, s, e):
                n = b * 2 + (e + 1)
                pe.wait_ge(s_nTl, n)
                pe.wait_ge(s_nT, n)
                h = slice(e * HW, (e + 1) * HW)
                three(WB[e], Whi[:, :], Wlo[:, :], nTh[:, s, h], nTl[:, s, h]).then_inc(s_U, 1)

            def values(b, e):
                n = b * 2 + (e + 1)
                pe.wait_ge(s_uTl, n)
                for t in range(HT):
                    k = e * HT + t
                    last = pe.matmul(WB[e][:, t * C:(t + 1) * C], nT[:, k * C:(k + 1) * C], Ac[:, :],
                                     start=True, stop=True)
                last.then_inc(s_H, 1)

            def rows(b, e, freed):
                pe.wait_ge(s_ot, b * 2 + (e + 1))
                if freed is not None:
                    pe.wait_ge(*freed)
                for t in range(HT):
                    last = pe.transpose(EB[e][:, t * C:(t + 1) * C], OT[:, t * C:(t + 1) * C], ident[:, :])
                last.then_inc(s_E, 1)

            def logits(b, s, k, first):
                e, m = divmod(k, TT)
                if not (first and k < SB):
                    pe.wait_ge(s_pl, b * UN + (k + 1 - SB))
                h, t = slice(e * HW, (e + 1) * HW), slice(m * C, (m + 1) * C)
                three(SL[k % SB], nTh[:, s, t], nTl[:, s, t], uTh[:, s, h], uTl[:, s, h]).then_inc(s_log, 1)

            def attend(b, s, k, first):
                e, m = divmod(k, TT)
                if m == 0 and not first:
                    pe.wait_ge(s_ot, b * 2 + (e - 1))
                if k == 0:
                    pe.wait_ge(s_hl, b * 2 + 2)
                pe.wait_ge(s_pl, b * UN + (k + 1))
                three(OO[e], hh[:, s, m, :], hl[:, s, m, :], Ph[:, k % PB, :], Pl[:, k % PB, :],
                      start=m == 0, stop=m == TT - 1).then_inc(s_av, 1)

            def image(b, s, first=False, last=False):
                for k in range(UN):
                    logits(b, s, k, first)
                    if k >= LAG:
                        attend(b, s, k - LAG, first)
                    elif not first:
                        attend(b - 1, 1 - s, UN + k - LAG, False)
                    if k == 3 and not first:
                        rows(b - 1, 1, (s_h, b * 2 + 1))
                    if k == 9 and not last:
                        transpose_tokens(b + 1, 0, (s_h, 1) if first else (s_y, b * 2))
                        transpose_tokens(b + 1, 1, (s_h, 2) if first else (s_y, b * 2 - 1))
                    if k == 11 and not last:
                        queries(b + 1, 1 - s, 0)
                        queries(b + 1, 1 - s, 1)
                    if k == 12 and not last:
                        values(b + 1, 0)
                    if k == 13 and not last:
                        values(b + 1, 1)
                    if k == 15:
                        rows(b, 0, (s_y, b * 2 - 1) if last else (s_h, b * 2 + 4))

            def prepare(b, freed):
                for e in (0, 1):
                    transpose_tokens(b, e, freed)
                for e in (0, 1):
                    queries(b, 0, e)
                for e in (0, 1):
                    values(b, e)

            def attention():
                prepare(0, None)
                image(0, 0, first=True)
                image(1, 1)
                with pe.Fori(1, B // 2 - 1) as i:
                    image(i * 2, 0)
                    image(i * 2 + 1, 1)
                image(B - 2, 0)
                image(B - 1, 1, last=True)
                for k in range(UN - LAG, UN):
                    attend(B - 1, 1, k, False)
                rows(B - 1, 1, (s_y, 2 * (B - 1)))

            def general():
                def general_image(b, first):
                    prepare(b, None if first else (s_y, b * 2))
                    pe.wait_ge(s_hl, b * 2 + 2)
                    for t in range(TT):
                        n = b * TT + t
                        if not (first and t == 0):
                            pe.wait_ge(g_exp, n)
                        if t == 0:
                            pe.wait_ge(s_uTl, b * 2 + 2)
                        q = slice(t * C, (t + 1) * C)
                        for e in (0, 1):
                            h = slice(e * HW, (e + 1) * HW)
                            last = three(SL[e], uTh[:, 0, q], uTl[:, 0, q], nTh[:, 0, h], nTl[:, 0, h])
                        last.then_inc(g_log, 1)
                        pe.wait_ge(g_exp, n + 1)
                        for e in (0, 1):
                            if not (first and t == 0):
                                pe.wait_ge(g_cp, n * 2 + (e - 1))
                            for k in range(HT):
                                last = pe.transpose(SL[2 + e][:, k * C:(k + 1) * C], tok[:, e * HT + k, :],
                                                    ident[:, :])
                            last.then_inc(g_tr, 1)
                        pe.wait_ge(g_cp, n * 2 + 2)
                        e, k = divmod(t, HT)
                        if k == 0 and not first:
                            pe.wait_ge(s_ot, b * 2 + (e - 1))
                        o = OO[e][:, k * C:(k + 1) * C]
                        for m in range(TT):
                            pt = nT[:, m * C:(m + 1) * C]
                            pe.matmul(o, hh[:, 0, m, :].bitcast(F32), pt, start=m == 0, stop=False)
                            last = pe.matmul(o, hl[:, 0, m, :].bitcast(F32), pt, start=False, stop=m == TT - 1)
                        last.then_inc(g_av, 1)
                    for e in (0, 1):
                        rows(b, e, (s_h, b * 2 + 2))

                general_image(0, True)
                with pe.Fori(1, B) as b:
                    general_image(b, False)

            pe.wait_ge(s_flag, 1)
            bounded = pe.value_load(flag[0:1, 0:1], min_val=0, max_val=1)
            with pe.If(bounded == 1):
                attention()
            with pe.Else():
                general()


def kernel(x, L0_conv_accumulators, L1_conv_global_feat, L1_conv_pos, L1_conv_adj_w, L1_conv_affine_w,
           L1_conv_affine_b, L1_conv_ln_g, L1_conv_ln_b):
    import concourse.bacc as bacc
    from concourse.bass_utils import run_bass_kernel_spmd

    arrays = {
        "x": np.asarray(x).reshape(B, Q, J * C).transpose(1, 0, 2).reshape(P, J * C),
        "acc": np.asarray(L0_conv_accumulators).reshape(Q, NCH, CJ, C, C).transpose(1, 3, 0, 2, 4)
        .reshape(NCH, C, Q * CJ * C),
        "adj_w": np.asarray(L1_conv_adj_w),
        "aff_w": np.asarray(L1_conv_affine_w),
        "aff_b": np.asarray(L1_conv_affine_b),
        "ln_g": np.asarray(L1_conv_ln_g),
        "ln_b": np.asarray(L1_conv_ln_b),
    }
    arrays = {k: np.ascontiguousarray(v) for k, v in arrays.items()}
    nc = bacc.Bacc("TRN2", target_bir_lowering=False, num_devices=1)
    ins = [nc.dram_tensor(k, v.shape, F32, kind="ExternalInput").ap() for k, v in arrays.items()]
    stat_dram = nc.dram_tensor("group_stats", (B, 2, G), F32, kind="Internal").ap()
    out = nc.dram_tensor("out", (B, NPOS, C), F32, kind="ExternalOutput").ap()
    build(nc, *ins, stat_dram, out)
    r = run_bass_kernel_spmd(nc, [arrays], core_ids=[0])
    return r.results[0]["out"].reshape(B, 32, 32, C)
```

```python
from contextlib import ExitStack

import concourse.bass as bass
import numpy as np
from concourse import mybir

F32 = mybir.dt.float32
F32R = mybir.dt.float32r
I32 = mybir.dt.int32
ALU = mybir.AluOpType
ACT = mybir.ActivationFunctionType
AX = mybir.AxisListType

P = 128
B = 32
NPOS = 1024
C = 128
G = 32
GC = C // G
Q = P // B
J = NPOS // Q
GN_EPS, LN_EPS, NORM_MIN, SLOPE, SHARP = 1e-5, 1e-5, 1e-12, 0.01, 5.0

CJ = 4
CW = CJ * C
NCH = J // CJ
WS = 4
ZS = 4
AHEAD = 3
U0 = 8
SP0 = 4
SP1 = NCH // U0
GPC = G // U0

TT = NPOS // P
HT = TT // 2
HW = HT * C
UN = 2 * TT
SB = 4
PB = 3
SLOT = [k % PB for k in range(UN - 1)] + [1]
SINCE = [next(d for d in range(1, UN) if SLOT[k - d] == SLOT[k]) for k in range(UN)]
LAG = 3
LIMIT = 64.0


def build(nc, x, acc, adj_w, aff_w, aff_b, ln_g, ln_b, stat_dram, out):
    ctx = ExitStack()
    with ctx:
        def sem(name):
            return ctx.enter_context(nc.semaphore(name))

        def sb(name, shape, dt=F32, c=ctx):
            return c.enter_context(nc.sbuf_tensor(name, shape, dt))

        X = sb("X", [P, J, C])
        ident = sb("ident", [P, P])
        Ac = sb("Ac", [P, C])
        b1 = sb("b1", [P, C])
        gB = sb("gB", [P, C])
        lbB = sb("lbB", [P, C])
        Whi = sb("Whi", [P, C], F32R)
        Wlo = sb("Wlo", [P, C], F32R)
        half_p = sb("half_p", [P, TT])
        half_n = sb("half_n", [P, G])
        MR = sb("MR", [P, 2, G])
        flag = sb("flag", [1, 1], I32)

        l0 = ExitStack()
        Wt = sb("Wt", [P, WS, Q, CJ, C], c=l0)
        Z = sb("Z", [P, ZS, CJ, C], c=l0)
        E = sb("E", [P, 2, CJ, C], c=l0)
        ET = sb("ET", [P, 2, CJ, C], c=l0)
        LP = sb("LP", [P, 2, CJ, C], c=l0)
        LS = sb("LS", [P, 2, CJ, C], c=l0)
        nmx = sb("nmx", [P, ZS, CJ], c=l0)
        st = sb("st", [P, SP1, G, 6], c=l0)
        dev = sb("dev", [P, G, SP1, 2], c=l0)
        gsum = sb("gsum", [P, G], c=l0)
        gvar = sb("gvar", [P, G], c=l0)
        col = sb("col", [P, 1], c=l0)
        mcol = sb("mcol", [P, 2], c=l0)
        ones = sb("ones", [P, B], c=l0)
        same_image = sb("same_image", [P, P], c=l0)
        adj_sb = sb("adj_sb", [P, C], c=l0)
        aff_sb = sb("aff_sb", [P, C], c=l0)
        l0.close()
        l1 = ExitStack()
        tok = sb("tok", [P, TT, C], c=l1)
        res = sb("res", [P, HT, C], c=l1)
        nTh = sb("nTh", [P, 2, NPOS], F32R, l1)
        nTl = sb("nTl", [P, 2, NPOS], F32R, l1)
        uTh = sb("uTh", [P, 3, HW], F32R, l1)
        uTl = sb("uTl", [P, 3, HW], F32R, l1)
        hh = sb("hh", [P, 2, TT, C], F32R, l1)
        hl = sb("hl", [P, 2, TT, C], F32R, l1)
        Ph = sb("Ph", [P, PB, HW], F32R, l1)
        Pl = sb("Pl", [P, PB, HW], F32R, l1)
        nT = sb("nT", [P, NPOS], c=l1)
        hf = sb("hf", [P, HT, C], c=l1)
        OT = sb("OT", [P, HW], c=l1)
        Y = sb("Y", [P, 2, HT, C], c=l1)
        YQ = OT[:, :].rearrange("p (t c) -> p t c", c=C)
        mrb = sb("mrb", [P, 2, G], c=l1)
        n2 = sb("n2", [P, TT], c=l1)
        nrm = sb("nrm", [P, 2, TT], c=l1)
        junk = sb("junk", [P, 2, C], c=l1)
        rn = sb("rn", [P, TT], c=l1)
        lastc = sb("lastc", [P, HT], c=l1)
        rs = sb("rs", [P, HT], c=l1)
        vs = sb("vs", [P, HT], c=l1)
        fac = sb("fac", [P, HT], c=l1)
        den = sb("den", [P, HT], c=l1)
        gmx = sb("gmx", [P, 1], c=l1)
        gnm = sb("gnm", [P, 1], c=l1)
        l1.close()

        PS = ctx.enter_context(nc.psum_tensor("PS", [P, 8, 512], F32))
        TP = [PS[:, i, :] for i in (0, 1)]
        PP = [PS[:, i, :] for i in (2, 3)]
        SS = [PS[:, i, :] for i in (4, 5)]
        MISC = PS[:, 6, :]
        SL = [PS[:, i, :] for i in range(SB)]
        OO = [PS[:, i, :] for i in (4, 5)]
        WB = [PS[:, i, :] for i in (6, 7)]

        s_par = sem("s_par")
        s_const = sem("s_const")
        s_wsplit = sem("s_wsplit")
        s_afft = sem("s_afft")
        s_ac = sem("s_ac")
        s_sq = sem("s_sq")
        s_norm = sem("s_norm")
        s_flag = sem("s_flag")
        s_x = [sem(f"s_load{i}") for i in range(SP0)]
        s_w = [sem(f"s_weights{i}") for i in range(WS)]
        s_bn = sem("s_bn")
        s_st = sem("s_st")
        s_gs = sem("s_gs")
        s_gp = sem("s_gp")
        s_zc = sem("s_zc")
        s_z = sem("s_z")
        s_min = sem("s_min")
        s_e = sem("s_e")
        s_tr = sem("s_tr")
        s_et = sem("s_et")
        s_prod = sem("s_prod")
        s_ln = sem("s_ln")
        s_lw = sem("s_lw")
        s_x1 = sem("s_x1")
        s_stout = sem("s_stout")
        s_mrb = sem("s_mrb")
        s_tok = sem("s_tok")
        s_free = sem("s_free")
        s_res = sem("s_res")
        s_out = [sem(f"s_out{i}") for i in (0, 1)]
        s_cent = sem("s_cent")
        s_gn = sem("s_gn")
        s_sqr = sem("s_sqr")
        s_root = sem("s_root")
        s_nmax = sem("s_nmax")
        s_rn = sem("s_rn")
        s_unit = sem("s_unit")
        s_T = sem("s_T")
        s_nTh = sem("s_nTh")
        s_nT = sem("s_nT")
        s_nTl = sem("s_nTl")
        s_U = sem("s_U")
        s_uTh = sem("s_uTh")
        s_uTl = sem("s_uTl")
        s_H = sem("s_H")
        s_h = sem("s_h")
        s_hh = sem("s_hh")
        s_hl = sem("s_hl")
        s_log = sem("s_log")
        s_exp = sem("s_exp")
        s_ph = sem("s_ph")
        s_pl = sem("s_pl")
        s_av = sem("s_av")
        s_ot = sem("s_ot")
        s_E = sem("s_E")
        s_y = sem("s_y")
        s_sum = sem("s_sum")
        s_den = sem("s_den")
        s_last = sem("s_last")
        s_yq = sem("s_yq")
        s_v = sem("s_v")
        s_isd = sem("s_isd")
        s_fac = sem("s_fac")
        s_y1 = sem("s_y1")
        s_y2 = sem("s_y2")
        s_y3 = sem("s_y3")
        s_y4 = sem("s_y4")
        g_log = sem("g_log")
        g_max = sem("g_max")
        g_neg = sem("g_neg")
        g_exp = sem("g_exp")
        g_tr = sem("g_tr")
        g_cp = sem("g_cp")
        g_av = sem("g_av")

        NST = 8
        NV = 5
        NCONST = 5 + 1 + 2 * Q - 1
        block = ctx.enter_context(nc.Block())
        out_v = out.rearrange("b (p t) c -> b p t c", t=TT)

        @block.sync
        def _(sp):
            sp.dma_start(adj_sb[:, :], adj_w).then_inc(s_par, 16)
            sp.dma_start(aff_sb[:, :], aff_w).then_inc(s_par, 16)
            for t, v in ((b1, aff_b), (gB, ln_g), (lbB, ln_b)):
                sp.dma_start(t[:, :], v.rearrange("(o c) -> o c", o=1).broadcast_to([P, C])).then_inc(s_par, 16)
            xj = J // SP0
            for i in range(SP0):
                sp.dma_start(X[:, i * xj:(i + 1) * xj, :], x[:, i * xj * C:(i + 1) * xj * C]
                             .rearrange("p (j c) -> p j c", c=C)).then_inc(s_x[i], 16)

            def load_weights(ch, slot, nth, wait):
                if wait:
                    sp.wait_ge(s_prod, nth)
                sp.dma_start(Wt[:, slot, :, :, :], acc[ch, :, :].rearrange(
                    "k (q i s) -> k q i s", q=Q, i=CJ)).then_inc(s_w[slot], 16)

            for ch in range(WS):
                load_weights(ch, ch, 0, False)
            with sp.Fori(1, NCH // WS) as r:
                for slot in range(WS):
                    load_weights(r * WS + slot, slot, r * WS + slot - WS + 1, True)

            def gather(b):
                for q in range(Q):
                    r = q * B + b
                    sp.dma_start(tok[q * B:(q + 1) * B, :, :],
                                 X[r:r + 1, :, :].rearrange("o (p t) c -> o p (t c)", t=TT)).then_inc(s_tok, 16)

            def gather_stats(b):
                if b:
                    sp.wait_ge(s_gn, b)
                sp.dma_start(mrb[:, :, :], stat_dram[b:b + 1, :, :].broadcast_to([P, 2, G])).then_inc(s_mrb, 16)

            def gather_residual(b, e):
                if 2 * b + e:
                    sp.wait_ge(s_y4, 2 * b + e)
                for q in range(Q):
                    r = q * B + b
                    sp.dma_start(res[q * B:(q + 1) * B, :, :],
                                 X[r:r + 1, :, :].rearrange("o (p e t) c -> o p e (t c)", e=2, t=HT)[:, :, e, :])\
                        .then_inc(s_res, 16)

            def store(b, e):
                sp.wait_ge(s_y4, 2 * b + e + 1)
                sp.dma_start(out_v[b, :, e * HT:(e + 1) * HT, :], Y[:, e, :, :]).then_inc(s_out[e], 16)

            sp.wait_ge(s_x1, NCH)
            gather(0)
            gather_residual(0, 0)
            sp.wait_ge(s_gp, 2)
            sp.dma_start(stat_dram, MR[0:B, :, :]).then_inc(s_stout, 16)
            sp.wait_ge(s_stout, 16)
            gather_stats(0)
            sp.wait_ge(s_flag, 1)
            bounded = sp.value_load(flag[0:1, 0:1], min_val=0, max_val=1)
            with sp.If(bounded == 1):
                gather_stats(1)
                sp.wait_ge(s_T, 2)
                gather(1)
                for b in range(B):
                    if b + 2 < B:
                        gather_stats(b + 2)
                        sp.wait_ge(s_T, 2 * (b + 2))
                        gather(b + 2)
                    if b:
                        store(b - 1, 0)
                        gather_residual(b - 1, 1)
                        store(b - 1, 1)
                        gather_residual(b, 0)
                store(B - 1, 0)
                gather_residual(B - 1, 1)
                store(B - 1, 1)
            with sp.Else():
                for b in range(B):
                    store(b, 0)
                    gather_residual(b, 1)
                    store(b, 1)
                    if b + 1 < B:
                        sp.wait_ge(s_free, b + 1)
                        gather(b + 1)
                        gather_stats(b + 1)
                        gather_residual(b + 1, 0)
            sp.wait_ge(s_out[0], 16 * B)
            sp.wait_ge(s_out[1], 16 * B)

        @block.gpsimd
        def _(pool):
            n = 0
            for t, v in ((ident, 0.0), (same_image, 0.0), (ones, 1.0), (half_p, 0.5), (half_n, -0.5)):
                pool.memset(t[:, :], v).then_inc(s_const, 1)
                n += 1
            for t, d in [(ident, 0)] + [(same_image, k * B) for k in range(1 - Q, Q)]:
                pool.wait_ge(s_const, n)
                pool.affine_select(out=t[:, :], in_=t[:, :], compare_op=ALU.not_equal, fill=1.0, base=-d,
                                   pattern=[[-1, P]], channel_multiplier=1).then_inc(s_const, 1)
                n += 1
            assert n == NCONST

            def inverse_deviation(turn):
                pool.wait_ge(s_st, NST * (turn + 1))
                pool.tensor_tensor(MR[:, 1, :], gvar[:, :], half_n[:, :], ALU.pow).then_inc(s_gp, 1)

            def normalise(c, u, first):
                xc = X[:, bass.ds(c * CJ, CJ), :].rearrange("p j (g k) -> p j g k", k=GC)
                z = Z[:, u % ZS, :, :].rearrange("p j (g k) -> p j g k", k=GC)
                if not first:
                    pool.wait_ge(s_e, c - ZS + 1)
                pool.tensor_tensor(z, MR[:, 0, :].unsqueeze(1).unsqueeze(3).broadcast_to([P, CJ, G, GC]), xc,
                                   ALU.subtract).then_inc(s_zc, 1)
                pool.wait_ge(s_zc, c + 1)
                pool.tensor_tensor(z, z, MR[:, 1, :].unsqueeze(1).unsqueeze(3).broadcast_to([P, CJ, G, GC]),
                                   ALU.mult).then_inc(s_z, 1)

            inverse_deviation(0)
            pool.wait_ge(s_gp, 1)
            for c in range(ZS):
                normalise(c, c, True)
            with pool.Fori(1, NCH // ZS) as i:
                for u in range(ZS):
                    normalise(i * ZS + u, u, False)
            inverse_deviation(1)

            def group_norm(b):
                t = tok[:, :, :].rearrange("p t (g k) -> p t g k", k=GC)
                pool.wait_ge(s_mrb, b * 16 + 16)
                pool.wait_ge(s_tok, b * (16 * Q) + 16 * Q)
                pool.tensor_tensor(t, t, mrb[:, 0, :].unsqueeze(1).unsqueeze(3).broadcast_to([P, TT, G, GC]),
                                   ALU.subtract).then_inc(s_cent, 1)
                pool.wait_ge(s_cent, b + 1)
                pool.tensor_tensor(t, t, mrb[:, 1, :].unsqueeze(1).unsqueeze(3).broadcast_to([P, TT, G, GC]),
                                   ALU.mult).then_inc(s_gn, 1)

            def root(b, s):
                pool.wait_ge(s_sqr, (b + 1) * TT)
                pool.tensor_tensor(nrm[:, s, :], n2[:, :], half_p[:, :], ALU.pow).then_inc(s_root, 1)

            def unit(b):
                pool.wait_ge(s_rn, b + 1)
                pool.tensor_tensor(tok[:, :, :], tok[:, :, :], rn[:, :].unsqueeze(2).broadcast_to([P, TT, C]),
                                   ALU.mult).then_inc(s_unit, 1)

            def squares(b, e):
                pool.wait_ge(s_last, b * 2 + (e + 1))
                pool.tensor_tensor(YQ[:, :, :], Y[:, e, :, :], Y[:, e, :, :], ALU.mult).then_inc(s_yq, 1)

            def inverse_sd(b, e):
                pool.wait_ge(s_v, (b * 2 + (e + 1)) * NV)
                pool.tensor_tensor(vs[:, :], vs[:, :], half_n[:, 0:HT], ALU.pow).then_inc(s_isd, 1)

            def add_beta(b, e):
                pool.wait_ge(s_y1, b * 2 + (e + 1))
                pool.tensor_tensor(Y[:, e, :, :], Y[:, e, :, :], lbB[:, :].unsqueeze(1).broadcast_to([P, HT, C]),
                                   ALU.add).then_inc(s_y2, 1)

            def add_residual(b, e):
                pool.wait_ge(s_y3, b * 2 + (e + 1))
                pool.wait_ge(s_res, (b * 2 + (e + 1)) * (16 * Q))
                pool.tensor_tensor(Y[:, e, :, :], Y[:, e, :, :], res[:, :, :], ALU.add).then_inc(s_y4, 1)

            def image(b, s, first=False, last=False, late=False):
                if not last:
                    root(b + 1, 1 - s)
                    unit(b + 1)
                if not first:
                    squares(b - 1, 0)
                    inverse_sd(b - 1, 0)
                    add_beta(b - 1, 0)
                    add_residual(b - 1, 0)
                    squares(b - 1, 1)
                    inverse_sd(b - 1, 1)
                if not (last or late):
                    group_norm(b + 2)
                if not first:
                    add_beta(b - 1, 1)
                    add_residual(b - 1, 1)

            def attention():
                group_norm(0)
                root(0, 0)
                unit(0)
                group_norm(1)
                image(0, 0, first=True)
                image(1, 1)
                with pool.Fori(1, B // 2 - 1) as i:
                    image(i * 2, 0)
                    image(i * 2 + 1, 1)
                image(B - 2, 0, late=True)
                image(B - 1, 1, last=True)
                for e in (0, 1):
                    squares(B - 1, e)
                    inverse_sd(B - 1, e)
                    add_beta(B - 1, e)
                    add_residual(B - 1, e)

            def general():
                with pool.Fori(0, B) as b:
                    group_norm(b)
                    root(b, 0)
                    unit(b)
                    for e in (0, 1):
                        squares(b, e)
                        inverse_sd(b, e)
                        add_beta(b, e)
                        add_residual(b, e)

            pool.wait_ge(s_flag, 1)
            bounded = pool.value_load(flag[0:1, 0:1], min_val=0, max_val=1)
            with pool.If(bounded == 1):
                attention()
            with pool.Else():
                general()

        @block.scalar
        def _(act):
            act.preload_act_table_set("natural_log_exp_and_others")
            act.wait_ge(s_par, 16 * 5)
            act.activation(LP[:, 0, 0, :], adj_sb[:, :], ACT.Square, accum_out=col[:, :]).then_inc(s_sq, 1)

            def exps(c, u):
                act.wait_ge(s_min, c + 1)
                for i in range(CJ):
                    last = act.activation(E[:, u % 2, i, :], Z[:, u % ZS, i, :], ACT.Exp,
                                          bias=nmx[:, u % ZS, i:i + 1], scale=-1.0)
                last.then_inc(s_e, 1)

            def logs(c, u, early=False):
                act.wait_ge(s_prod, c + 1)
                if early:
                    act.wait_ge(s_sq, 1)
                else:
                    act.wait_ge(s_x1, c - 1)
                act.activation(LP[:, u % 2, :, :], PP[u % 2].rearrange("p (i c) -> p i c", c=C), ACT.Ln)
                act.activation(LS[:, u % 2, :, :], SS[u % 2].rearrange("p (i c) -> p i c", c=C), ACT.Ln)\
                    .then_inc(s_ln, 1)

            def step(c, u, first=False, last=False):
                if not last:
                    if not first:
                        act.wait_ge(s_tr, c)
                    exps(c + 1, u + 1)
                act.wait_ge(s_tr, c + 1)
                act.activation(ET[:, u % 2, :, :], TP[u % 2].rearrange("p (i c) -> p i c", c=C), ACT.Copy)\
                    .then_inc(s_et, 1)
                if not first:
                    logs(c - 1, u - 1, early=isinstance(c, int) and c <= 2)

            exps(0, 0)
            for c in range(U0):
                step(c, c, first=c == 0)
            with act.Fori(1, NCH // U0 - 1) as i:
                for u in range(U0):
                    step(i * U0 + u, U0 + u)
            for c in range(NCH - U0, NCH):
                step(c, c, last=c == NCH - 1)
            logs(NCH - 1, NCH - 1)

            def token_squares(b, tiles, first=False):
                act.wait_ge(s_gn, b + 1)
                if not first:
                    act.wait_ge(s_root, b)
                for t in tiles:
                    if t >= 2 or not first:
                        act.wait_ge(s_sqr, b * TT + (t - 1))
                    act.activation(junk[:, t % 2, :], tok[:, t, :], ACT.Square, accum_out=n2[:, t:t + 1])\
                        .then_inc(s_sqr, 1)

            def tokens_T(b, s, e, freed):
                act.wait_ge(s_T, b * 2 + (e + 1))
                if freed is not None:
                    act.wait_ge(*freed)
                act.activation(nT[:, e * HW:(e + 1) * HW], WB[e], ACT.Copy).then_inc(s_nT, 1)
                act.activation(nTh[:, s, e * HW:(e + 1) * HW], WB[e], ACT.Copy).then_inc(s_nTh, 1)

            def queries_T(b, s, e, freed=None):
                act.wait_ge(s_U, b * 2 + (e + 1))
                if freed is not None:
                    act.wait_ge(*freed)
                act.activation(uTh[:, e * (1 + s), :], WB[e], ACT.Copy).then_inc(s_uTh, 1)

            def take_output(b, e, made, first=False):
                act.wait_ge(*made)
                if not first:
                    act.wait_ge(s_v, (b * 2 + e) * NV)
                act.activation(OT[:, :], OO[e], ACT.Copy).then_inc(s_ot, 1)

            def take_rows(b, e, first=False):
                act.wait_ge(s_E, b * 2 + (e + 1))
                if not first:
                    act.wait_ge(s_out[e], b * 16)
                act.activation(Y[:, e, :, :], WB[e].rearrange("p (t c) -> p t c", c=C), ACT.Copy).then_inc(s_y, 1)

            def unit_step(b, k, first):
                sl = SL[k % SB]
                act.wait_ge(s_log, b * UN + (k + 1))
                if not (first and k < PB):
                    act.wait_ge(s_av, b * UN + (k + 1 - SINCE[k]))
                act.activation(Ph[:, SLOT[k], :], sl, ACT.Exp, scale=SHARP).then_inc(s_ph, 1)
                act.activation(sl, sl, ACT.Exp, scale=SHARP).then_inc(s_exp, 1)

            def image(b, s, first=False, second=False, last=False, late=False):
                for k in range(UN):
                    unit_step(b, k, first)
                    if k == 3 and not last:
                        tokens_T(b + 1, 1 - s, 0, None if first else (s_log, b * UN))
                    if k == 5 and not first:
                        take_output(b - 1, 1, (s_av, b * UN))
                    if k == 6 and not first:
                        take_rows(b - 1, 1, first=second)
                    if k == 7 and not last:
                        queries_T(b + 1, 1 - s, 0, (s_log, b * UN + TT))
                    if k == 8 and not last:
                        tokens_T(b + 1, 1 - s, 1, None)
                    if k == 11:
                        take_output(b, 0, (s_av, b * UN + TT), first=first)
                    if k == 12 and not last:
                        queries_T(b + 1, 1 - s, 1)
                    if k == 15:
                        take_rows(b, 0, first=first)
                    if k in (14, 15) and not (last or late):
                        token_squares(b + 2, range(HT) if k == 14 else range(HT, TT))

            def prepare(b):
                for e in (0, 1):
                    tokens_T(b, 0, e, None)
                for e in (0, 1):
                    queries_T(b, 0, e)

            def attention():
                token_squares(0, range(TT), first=True)
                prepare(0)
                token_squares(1, range(TT))
                image(0, 0, first=True)
                image(1, 1, second=True)
                with act.Fori(1, B // 2 - 1) as i:
                    image(i * 2, 0)
                    image(i * 2 + 1, 1)
                image(B - 2, 0, late=True)
                image(B - 1, 1, last=True)
                take_output(B - 1, 1, (s_av, B * UN))
                take_rows(B - 1, 1)

            def general():
                def general_image(b, first):
                    token_squares(b, range(TT), first)
                    prepare(b)
                    act.wait_ge(s_H, b * 2 + 2)
                    for t in range(TT):
                        act.wait_ge(g_neg, b * TT + (t + 1))
                        if t:
                            act.wait_ge(g_av, b * TT + t)
                        act.activation(tok[:, :, :].rearrange("p t c -> p (t c)"),
                                       PS[:, 0:2, :].rearrange("p a c -> p (a c)"), ACT.Exp,
                                       bias=gnm[:, :], scale=SHARP).then_inc(g_exp, 1)
                        for e in (0, 1):
                            act.wait_ge(g_tr, b * (2 * TT) + (2 * t + e + 1))
                            act.activation(nT[:, e * HW:(e + 1) * HW], SL[2 + e], ACT.Copy).then_inc(g_cp, 1)
                    for e in (0, 1):
                        take_output(b, e, (g_av, b * TT + (e + 1) * HT), first=first and e == 0)
                        take_rows(b, e, first=first)

                general_image(0, True)
                with act.Fori(1, B) as b:
                    general_image(b, False)

            act.wait_ge(s_flag, 1)
            bounded = act.value_load(flag[0:1, 0:1], min_val=0, max_val=1)
            with act.If(bounded == 1):
                attention()
            with act.Else():
                general()

        @block.vector
        def _(dve):
            dve.wait_ge(s_par, 16 * 5)
            dve.tensor_copy(Whi[:, :], adj_sb[:, :]).then_inc(s_wsplit, 1)
            dve.wait_ge(s_wsplit, 1)
            dve.tensor_tensor(Wlo[:, :], adj_sb[:, :], Whi[:, :].bitcast(F32), ALU.subtract).then_inc(s_wsplit, 1)
            dve.wait_ge(s_afft, 1)
            dve.reduce_sum(mcol[:, 0:1], PP[0][:, 0:C], AX.X).then_inc(s_ac, 1)
            dve.reduce_sum(mcol[:, 1:2], b1[:, :], AX.X).then_inc(s_ac, 1)
            dve.wait_ge(s_ac, 2)
            dve.tensor_scalar(mcol[:, :], mcol[:, :], 1.0 / C, None, ALU.mult).then_inc(s_ac, 1)
            dve.wait_ge(s_ac, 3)
            dve.tensor_scalar(Ac[:, :], PP[0][:, 0:C], mcol[:, 0:1], None, ALU.subtract).then_inc(s_ac, 1)
            dve.tensor_scalar(b1[:, :], b1[:, :], mcol[:, 1:2], None, ALU.subtract).then_inc(s_ac, 1)
            dve.wait_ge(s_ac, 5)
            dve.memset(Ac[:, C - 1:C], 0.0).then_inc(s_ac, 1)
            dve.memset(b1[:, C - 1:C], 1.0).then_inc(s_ac, 1)
            dve.wait_ge(s_norm, 1)
            dve.tensor_scalar(flag[0:1, 0:1], PP[1][0:1, 0:1], SHARP * SHARP, LIMIT * LIMIT, ALU.mult, ALU.is_le)\
                .then_inc(s_flag, 1)

            def piece_stats(m, pieces, groups):
                for g in groups:
                    last = dve.bn_stats(st[:, m, g, :] if isinstance(m, int) else st[:, bass.ds(m, 1), g, :],
                                        X[:, bass.ds(m * (J // pieces), J // pieces), g * GC:(g + 1) * GC])
                return last

            def statistics(turn, pieces):
                parts = st[:, 0:pieces, :, :].rearrange("p m g (e s) -> p g m e s", s=3)
                n = J // pieces * GC // 2
                d = dev[:, :, 0:pieces, :]
                at = NST * turn
                dve.wait_ge(s_bn, SP0 + SP1 * turn)
                dve.tensor_reduce(gsum[:, :], parts[:, :, :, :, 1], AX.XY, ALU.add).then_inc(s_st, 1)
                dve.wait_ge(s_gs, 2 * turn + 1)
                dve.tensor_scalar(MR[:, 0, :], MISC[:, 0:G], 1.0 / (2 * pieces * Q), None, ALU.mult).then_inc(s_st, 1)
                dve.wait_ge(s_st, at + 2)
                dve.tensor_tensor(d, parts[:, :, :, :, 1],
                                  MR[:, 0, :].unsqueeze(2).unsqueeze(3).broadcast_to([P, G, pieces, 2]),
                                  ALU.subtract).then_inc(s_st, 1)
                dve.wait_ge(s_st, at + 3)
                dve.tensor_tensor(d, d, d, ALU.mult).then_inc(s_st, 1)
                dve.wait_ge(s_st, at + 4)
                dve.tensor_reduce(gvar[:, :], d, AX.XY, ALU.add).then_inc(s_st, 1)
                dve.tensor_reduce(gsum[:, :], parts[:, :, :, :, 2], AX.XY, ALU.add).then_inc(s_st, 1)
                dve.wait_ge(s_st, at + 6)
                dve.scalar_tensor_tensor(out=gsum[:, :], in0=gvar[:, :], scalar=float(n), in1=gsum[:, :],
                                         op0=ALU.mult, op1=ALU.add).then_inc(s_st, 1)
                dve.wait_ge(s_gs, 2 * turn + 2)
                dve.tensor_scalar(gvar[:, :], MISC[:, G:2 * G], 1.0 / (NPOS * GC), GN_EPS, ALU.mult, ALU.add)\
                    .then_inc(s_st, 1)

            for m in range(SP0):
                dve.wait_ge(s_x[m], 16)
                piece_stats(m, SP0, range(G)).then_inc(s_bn, 1)
            statistics(0, SP0)

            def minima(c, u):
                dve.wait_ge(s_z, c + 1)
                dve.tensor_reduce(nmx[:, u % ZS, :], Z[:, u % ZS, :, :], AX.X, ALU.min).then_inc(s_min, 1)

            def result(c, u):
                dve.wait_ge(s_ln, c + 1)
                for i in range(CJ):
                    last = dve.scalar_tensor_tensor(out=LP[:, u % 2, i, :], in0=LP[:, u % 2, i, :],
                                                    scalar=nmx[:, u % ZS, i:i + 1], in1=LS[:, u % 2, i, :],
                                                    op0=ALU.subtract, op1=ALU.subtract)
                last.then_inc(s_lw, 1)
                dve.wait_ge(s_lw, c + 1)
                xc = X[:, bass.ds(c * CJ, CJ), :]
                dve.tensor_tensor(xc, LP[:, u % 2, :, :], xc, ALU.add).then_inc(s_x1, 1)

            for c in range(AHEAD):
                minima(c, c)

            def chunks(i, first=False, last=False):
                if not first:
                    dve.wait_ge(s_x1, i * U0)
                for u in range(U0):
                    if not (last and u + AHEAD >= U0):
                        minima(i * U0 + (u + AHEAD), u + AHEAD)
                    result(i * U0 + u, u)
                    if not first:
                        done = piece_stats(i - 1, SP1, range(u * GPC, (u + 1) * GPC))
                if not first:
                    done.then_inc(s_bn, 1)

            chunks(0, first=True)
            with dve.Fori(1, NCH // U0 - 1) as i:
                chunks(i)
            chunks(NCH // U0 - 1, last=True)
            dve.wait_ge(s_x1, NCH)
            piece_stats(SP1 - 1, SP1, range(G)).then_inc(s_bn, 1)
            statistics(1, SP1)

            def inverse_norms(b, s):
                dve.wait_ge(s_root, b + 1)
                dve.tensor_scalar(nrm[:, s, :], nrm[:, s, :], NORM_MIN, None, ALU.max).then_inc(s_nmax, 1)
                dve.wait_ge(s_nmax, b + 1)
                dve.reciprocal(rn[:, :], nrm[:, s, :]).then_inc(s_rn, 1)

            def tokens_lower(b, s, e):
                dve.wait_ge(s_nTh, b * 2 + (e + 1))
                dve.tensor_tensor(nTl[:, s, e * HW:(e + 1) * HW], WB[e],
                                  nTh[:, s, e * HW:(e + 1) * HW].bitcast(F32), ALU.subtract).then_inc(s_nTl, 1)

            def queries_lower(b, s, e):
                dve.wait_ge(s_uTh, b * 2 + (e + 1))
                dve.tensor_tensor(uTl[:, e * (1 + s), :], WB[e], uTh[:, e * (1 + s), :].bitcast(F32),
                                  ALU.subtract).then_inc(s_uTl, 1)

            def values(b, s, e, first=False):
                n = b * 2 + (e + 1)
                dve.wait_ge(s_H, n)
                if not first:
                    dve.wait_ge(s_hl, n - 1)
                for t in range(HT):
                    last = dve.scalar_tensor_tensor(out=hf[:, t, :], in0=WB[e][:, t * C:(t + 1) * C],
                                                    scalar=nrm[:, s, e * HT + t:e * HT + t + 1], in1=b1[:, :],
                                                    op0=ALU.mult, op1=ALU.add)
                last.then_inc(s_h, 1)

            def values_parts(b, s, e, freed=None):
                n = b * 2 + (e + 1)
                half = slice(e * HT, (e + 1) * HT)
                if freed is not None:
                    dve.wait_ge(*freed)
                dve.wait_ge(s_h, n)
                dve.tensor_copy(hh[:, s, half, :], hf[:, :, :]).then_inc(s_hh, 1)
                dve.wait_ge(s_hh, n)
                dve.tensor_tensor(hl[:, s, half, :], hf[:, :, :], hh[:, s, half, :].bitcast(F32),
                                  ALU.subtract).then_inc(s_hl, 1)

            def release(left):
                dve.wait_ge(*left)
                dve.memset(gmx[:, :], 0.0).then_inc(s_free, 1)

            def weights_lower(b, k):
                dve.wait_ge(s_exp, b * UN + (k + 1))
                dve.tensor_tensor(Pl[:, SLOT[k], :], SL[k % SB], Ph[:, SLOT[k], :].bitcast(F32), ALU.subtract)\
                    .then_inc(s_pl, 1)

            def last_channel(b, e):
                n = b * 2 + (e + 1)
                dve.wait_ge(s_y, n)
                dve.tensor_reduce(lastc[:, :], Y[:, e, :, 0:C - 1], AX.X, ALU.add).then_inc(s_sum, 1)
                dve.tensor_copy(den[:, :], Y[:, e, :, C - 1]).then_inc(s_den, 1)
                dve.wait_ge(s_sum, n)
                dve.wait_ge(s_den, n)
                dve.tensor_scalar(Y[:, e, :, C - 1], lastc[:, :], -1.0, None, ALU.mult).then_inc(s_last, 1)

            def variance(b, e):
                n = b * 2 + (e + 1)
                at = (b * 2 + e) * NV
                dve.reciprocal(rs[:, :], den[:, :]).then_inc(s_v, 1)
                dve.wait_ge(s_yq, n)
                dve.reduce_sum(vs[:, :], YQ[:, :, :], AX.X).then_inc(s_v, 1)
                dve.wait_ge(s_v, at + 2)
                dve.scalar_tensor_tensor(out=vs[:, :], in0=vs[:, :], scalar=1.0 / C, in1=rs[:, :],
                                         op0=ALU.mult, op1=ALU.mult).then_inc(s_v, 1)
                dve.wait_ge(s_v, at + 3)
                dve.tensor_tensor(vs[:, :], vs[:, :], rs[:, :], ALU.mult).then_inc(s_v, 1)
                dve.wait_ge(s_v, at + 4)
                dve.tensor_scalar(vs[:, :], vs[:, :], LN_EPS, None, ALU.add).then_inc(s_v, 1)

            def scale_rows(b, e):
                n = b * 2 + (e + 1)
                dve.wait_ge(s_isd, n)
                dve.tensor_tensor(fac[:, :], vs[:, :], rs[:, :], ALU.mult).then_inc(s_fac, 1)
                dve.wait_ge(s_fac, n)
                for t in range(HT):
                    last = dve.scalar_tensor_tensor(out=Y[:, e, t, :], in0=Y[:, e, t, :], scalar=fac[:, t:t + 1],
                                                    in1=gB[:, :], op0=ALU.mult, op1=ALU.mult)
                last.then_inc(s_y1, 1)

            def leaky(b, e):
                dve.wait_ge(s_y2, b * 2 + (e + 1))
                y = Y[:, e, :, :]
                dve.scalar_tensor_tensor(out=y, in0=y, scalar=SLOPE, in1=y, op0=ALU.mult, op1=ALU.max)\
                    .then_inc(s_y3, 1)

            def image(b, s, first=False, last=False, late=False):
                for k in range(UN):
                    weights_lower(b, k)
                    if k == 0:
                        if not first:
                            last_channel(b - 1, 0)
                        if not last:
                            inverse_norms(b + 1, 1 - s)
                    if k == 1 and not first:
                        values(b, s, 1)
                    if k == 2 and not first:
                        values_parts(b, s, 1)
                    if k == 3 and not first:
                        variance(b - 1, 0)
                    if k == 4 and not last:
                        tokens_lower(b + 1, 1 - s, 0)
                    if k == 5 and not first:
                        scale_rows(b - 1, 0)
                    if k == 6 and not first:
                        leaky(b - 1, 0)
                    if k == 7 and not first:
                        last_channel(b - 1, 1)
                    if k == 8 and not last:
                        queries_lower(b + 1, 1 - s, 0)
                    if k == 9 and not last:
                        tokens_lower(b + 1, 1 - s, 1)
                    if k == 10 and not first:
                        variance(b - 1, 1)
                    if k == 11 and not first:
                        scale_rows(b - 1, 1)
                    if k == 12 and not last:
                        values(b + 1, 1 - s, 0)
                    if k == 13 and not last:
                        values_parts(b + 1, 1 - s, 0, None if first else (s_av, b * UN))
                    if k == 13 and not last:
                        queries_lower(b + 1, 1 - s, 1)
                    if k == 15 and not first:
                        leaky(b - 1, 1)

            def prepare(b, first):
                inverse_norms(b, 0)
                tokens_lower(b, 0, 0)
                tokens_lower(b, 0, 1)
                for e in (0, 1):
                    queries_lower(b, 0, e)
                    values(b, 0, e, first=first and e == 0)
                    values_parts(b, 0, e)

            def finish(b, e):
                last_channel(b, e)
                variance(b, e)
                scale_rows(b, e)
                leaky(b, e)

            def attention():
                prepare(0, True)
                image(0, 0, first=True)
                image(1, 1)
                with dve.Fori(1, B // 2 - 1) as i:
                    image(i * 2, 0)
                    image(i * 2 + 1, 1)
                image(B - 2, 0, late=True)
                image(B - 1, 1, last=True)
                finish(B - 1, 0)
                finish(B - 1, 1)

            def general():
                def general_image(b, first):
                    prepare(b, first)
                    for t in range(TT):
                        n = b * TT + (t + 1)
                        dve.wait_ge(g_log, n)
                        dve.reduce_max(gmx[:, :], PS[:, 0:2, :].rearrange("p a c -> p (a c)"), AX.X).then_inc(g_max, 1)
                        dve.wait_ge(g_max, n)
                        dve.tensor_scalar(gnm[:, :], gmx[:, :], -SHARP, None, ALU.mult).then_inc(g_neg, 1)
                    release((g_av, b * TT + TT))
                    for e in (0, 1):
                        finish(b, e)

                general_image(0, True)
                with dve.Fori(1, B) as b:
                    general_image(b, False)

            dve.wait_ge(s_flag, 1)
            bounded = dve.value_load(flag[0:1, 0:1], min_val=0, max_val=1)
            with dve.If(bounded == 1):
                attention()
            with dve.Else():
                general()

        @block.tensor
        def _(pe):
            pe.wait_ge(s_const, NCONST)
            pe.wait_ge(s_par, 16 * 5)
            pe.transpose(PP[0][:, 0:C], aff_sb[:, :], ident[:, :]).then_inc(s_afft, 1)
            pe.wait_ge(s_sq, 1)
            pe.matmul(PP[1][0:B, 0:1], ones[:, :], col[:, :], start=True, stop=True).then_inc(s_norm, 1)

            def sum_quarters(turn):
                for h in (0, 1):
                    pe.wait_ge(s_st, NST * turn + (1, 7)[h])
                    pe.matmul(MISC[:, h * G:(h + 1) * G], same_image[:, :], gsum[:, :], start=True, stop=True)\
                        .then_inc(s_gs, 1)

            sum_quarters(0)

            def transposes(c, u, first=False):
                pe.wait_ge(s_e, c + 1)
                if not first:
                    pe.wait_ge(s_et, c - 1)
                for i in range(CJ):
                    last = pe.transpose(TP[u % 2][:, i * C:(i + 1) * C], E[:, u % 2, i, :], ident[:, :])
                last.then_inc(s_tr, 1)

            def products(c, u, nth, first=False):
                w = Wt[:, u % WS, :, :, :]
                pe.wait_ge(s_w[u % WS], nth)
                if not first:
                    pe.wait_ge(s_ln, c - 1)
                for q in range(Q):
                    pe.matmul(SS[u % 2][q * B:(q + 1) * B, :], ones[:, :], w[:, q, :, :].rearrange("k i s -> k (i s)"),
                              start=True, stop=True)
                pe.wait_ge(s_et, c + 1)
                for i in range(CJ):
                    for q in range(Q):
                        last = pe.matmul(PP[u % 2][q * B:(q + 1) * B, i * C:(i + 1) * C],
                                         ET[:, u % 2, i, q * B:(q + 1) * B], w[:, q, i, :], start=True, stop=True)
                last.then_inc(s_prod, 1)

            def chunks(i, first=False, last=False):
                for u in range(U0):
                    if not (last and u == U0 - 1):
                        transposes(i * U0 + (u + 1), u + 1, first=first and u == 0)
                    products(i * U0 + u, u, i * (U0 // WS * 16) + (u // WS + 1) * 16, first=first and u < 2)

            transposes(0, 0, first=True)
            chunks(0, first=True)
            with pe.Fori(1, NCH // U0 - 1) as i:
                chunks(i)
            chunks(NCH // U0 - 1, last=True)
            sum_quarters(1)

            def three(out_, lh, ll, rh, rl, start=True, stop=True):
                pe.matmul(out_, lh, rh, start=start, stop=False)
                pe.matmul(out_, lh, rl, start=False, stop=False)
                return pe.matmul(out_, ll, rh, start=False, stop=stop)

            def transpose_tokens(b, e, freed):
                pe.wait_ge(s_unit, b + 1)
                if freed is not None:
                    pe.wait_ge(*freed)
                for t in range(HT):
                    last = pe.transpose(WB[e][:, t * C:(t + 1) * C], tok[:, e * HT + t, :], ident[:, :])
                last.then_inc(s_T, 1)

            def queries(b, s, e):
                n = b * 2 + (e + 1)
                pe.wait_ge(s_nTl, n)
                pe.wait_ge(s_nT, n)
                h = slice(e * HW, (e + 1) * HW)
                three(WB[e], Whi[:, :], Wlo[:, :], nTh[:, s, h], nTl[:, s, h]).then_inc(s_U, 1)

            def values(b, e):
                n = b * 2 + (e + 1)
                pe.wait_ge(s_uTl, n)
                for t in range(HT):
                    k = e * HT + t
                    last = pe.matmul(WB[e][:, t * C:(t + 1) * C], nT[:, k * C:(k + 1) * C], Ac[:, :],
                                     start=True, stop=True)
                last.then_inc(s_H, 1)

            def rows(b, e, freed):
                pe.wait_ge(s_ot, b * 2 + (e + 1))
                if freed is not None:
                    pe.wait_ge(*freed)
                for t in range(HT):
                    last = pe.transpose(WB[e][:, t * C:(t + 1) * C], OT[:, t * C:(t + 1) * C], ident[:, :])
                last.then_inc(s_E, 1)

            def logits(b, s, k, first):
                e, m = divmod(k, TT)
                if not (first and k < SB):
                    pe.wait_ge(s_pl, b * UN + (k + 1 - SB))
                t, u = slice(m * C, (m + 1) * C), e * (1 + s)
                three(SL[k % SB], nTh[:, s, t], nTl[:, s, t], uTh[:, u, :], uTl[:, u, :]).then_inc(s_log, 1)

            def attend(b, s, k, first):
                e, m = divmod(k, TT)
                if m == 0 and not first:
                    pe.wait_ge(s_ot, b * 2 + (e - 1))
                if k == 0:
                    pe.wait_ge(s_hl, b * 2 + 1)
                if k == HT:
                    pe.wait_ge(s_hl, b * 2 + 2)
                pe.wait_ge(s_pl, b * UN + (k + 1))
                three(OO[e], hh[:, s, m, :], hl[:, s, m, :], Ph[:, SLOT[k], :], Pl[:, SLOT[k], :],
                      start=m == 0, stop=m == TT - 1).then_inc(s_av, 1)

            def image(b, s, first=False, last=False, late=False):
                for k in range(UN):
                    logits(b, s, k, first)
                    if k >= LAG:
                        attend(b, s, k - LAG, first)
                    elif not first:
                        attend(b - 1, 1 - s, UN + k - LAG, False)
                    if k == 0 and not first:
                        values(b, 1)
                    if k == 3 and not last:
                        transpose_tokens(b + 1, 0, (s_h, 1) if first else (s_y, b * 2 - 1))
                    if k == 6 and not first:
                        rows(b - 1, 1, (s_h, b * 2 + 2))
                    if k == 7 and not last:
                        queries(b + 1, 1 - s, 0)
                    if k == 8 and not last:
                        transpose_tokens(b + 1, 1, (s_h, 2) if first else (s_y, b * 2))
                    if k == 11 and not last:
                        values(b + 1, 0)
                    if k == 12 and not last:
                        queries(b + 1, 1 - s, 1)
                    if k == 15:
                        rows(b, 0, (s_y, b * 2 - 1) if last else (s_h, b * 2 + 3))

            def prepare(b, freed):
                for e in (0, 1):
                    transpose_tokens(b, e, freed)
                for e in (0, 1):
                    queries(b, 0, e)
                    values(b, e)

            def attention():
                prepare(0, None)
                image(0, 0, first=True)
                image(1, 1)
                with pe.Fori(1, B // 2 - 1) as i:
                    image(i * 2, 0)
                    image(i * 2 + 1, 1)
                image(B - 2, 0, late=True)
                image(B - 1, 1, last=True)
                for k in range(UN - LAG, UN):
                    attend(B - 1, 1, k, False)
                rows(B - 1, 1, (s_y, 2 * (B - 1)))

            def general():
                def general_image(b, first):
                    prepare(b, None if first else (s_y, b * 2))
                    pe.wait_ge(s_hl, b * 2 + 2)
                    for t in range(TT):
                        n = b * TT + t
                        if not (first and t == 0):
                            pe.wait_ge(g_exp, n)
                        if t == 0:
                            pe.wait_ge(s_uTl, b * 2 + 2)
                        u, q = t // HT, slice(t % HT * C, (t % HT + 1) * C)
                        for e in (0, 1):
                            h = slice(e * HW, (e + 1) * HW)
                            last = three(SL[e], uTh[:, u, q], uTl[:, u, q], nTh[:, 0, h], nTl[:, 0, h])
                        last.then_inc(g_log, 1)
                        pe.wait_ge(g_exp, n + 1)
                        for e in (0, 1):
                            if not (first and t == 0):
                                pe.wait_ge(g_cp, n * 2 + (e - 1))
                            for k in range(HT):
                                last = pe.transpose(SL[2 + e][:, k * C:(k + 1) * C], tok[:, e * HT + k, :],
                                                    ident[:, :])
                            last.then_inc(g_tr, 1)
                        pe.wait_ge(g_cp, n * 2 + 2)
                        e, k = divmod(t, HT)
                        if k == 0 and not first:
                            pe.wait_ge(s_ot, b * 2 + (e - 1))
                        o = OO[e][:, k * C:(k + 1) * C]
                        for m in range(TT):
                            pt = nT[:, m * C:(m + 1) * C]
                            pe.matmul(o, hh[:, 0, m, :].bitcast(F32), pt, start=m == 0, stop=False)
                            last = pe.matmul(o, hl[:, 0, m, :].bitcast(F32), pt, start=False, stop=m == TT - 1)
                        last.then_inc(g_av, 1)
                    for e in (0, 1):
                        rows(b, e, (s_h, b * 2 + 2))

                general_image(0, True)
                with pe.Fori(1, B) as b:
                    general_image(b, False)

            pe.wait_ge(s_flag, 1)
            bounded = pe.value_load(flag[0:1, 0:1], min_val=0, max_val=1)
            with pe.If(bounded == 1):
                attention()
            with pe.Else():
                general()


def kernel(x, L0_conv_accumulators, L1_conv_global_feat, L1_conv_pos, L1_conv_adj_w, L1_conv_affine_w,
           L1_conv_affine_b, L1_conv_ln_g, L1_conv_ln_b):
    import concourse.bacc as bacc
    from concourse.bass_utils import run_bass_kernel_spmd

    arrays = {
        "x": np.asarray(x).reshape(B, Q, J * C).transpose(1, 0, 2).reshape(P, J * C),
        "acc": np.asarray(L0_conv_accumulators).reshape(Q, NCH, CJ, C, C).transpose(1, 3, 0, 2, 4)
        .reshape(NCH, C, Q * CJ * C),
        "adj_w": np.asarray(L1_conv_adj_w),
        "aff_w": np.asarray(L1_conv_affine_w),
        "aff_b": np.asarray(L1_conv_affine_b),
        "ln_g": np.asarray(L1_conv_ln_g),
        "ln_b": np.asarray(L1_conv_ln_b),
    }
    arrays = {k: np.ascontiguousarray(v) for k, v in arrays.items()}
    nc = bacc.Bacc("TRN2", target_bir_lowering=False, num_devices=1)
    ins = [nc.dram_tensor(k, v.shape, F32, kind="ExternalInput").ap() for k, v in arrays.items()]
    stat_dram = nc.dram_tensor("group_stats", (B, 2, G), F32, kind="Internal").ap()
    out = nc.dram_tensor("out", (B, NPOS, C), F32, kind="ExternalOutput").ap()
    build(nc, *ins, stat_dram, out)
    r = run_bass_kernel_spmd(nc, [arrays], core_ids=[0])
    return r.results[0]["out"].reshape(B, 32, 32, C)
```

```python
from contextlib import ExitStack

import concourse.bass as bass
import numpy as np
from concourse import mybir

F32 = mybir.dt.float32
F32R = mybir.dt.float32r
I32 = mybir.dt.int32
ALU = mybir.AluOpType
ACT = mybir.ActivationFunctionType
AX = mybir.AxisListType

P = 128
B = 32
NPOS = 1024
C = 128
G = 32
GC = C // G
GQ = G // 4
Q = P // B
J = NPOS // Q
GN_EPS, LN_EPS, NORM_MIN, SLOPE, SHARP = 1e-5, 1e-5, 1e-12, 0.01, 5.0

CJ = 4
HCJ = CJ // 2
CW = CJ * C
NCH = J // CJ
WS = 4
ZS = 4
MS = 8
AHEAD = 4
BEHIND = 6
U0 = 8
SP0 = 4
SP1 = NCH // U0
USKIP = 0

TT = NPOS // P
HT = TT // 2
HW = HT * C
UN = 2 * TT
SB = 4
PB = 3
SLOT = [k % PB for k in range(UN - 1)] + [1]
SINCE = [next(d for d in range(1, UN) if SLOT[k - d] == SLOT[k]) for k in range(UN)]
LAG = 3
LIMIT = 24.0


def build(nc, x, acc, adj_w, aff_w, aff_b, ln_g, ln_b, out):
    ctx = ExitStack()
    with ctx:
        def sem(name):
            return ctx.enter_context(nc.semaphore(name))

        def sb(name, shape, dt=F32, c=ctx):
            return c.enter_context(nc.sbuf_tensor(name, shape, dt))

        X = sb("X", [P, J, C])
        ident = sb("ident", [P, P])
        Ac = sb("Ac", [P, C])
        b1 = sb("b1", [P, C])
        gB = sb("gB", [P, C])
        lbB = sb("lbB", [P, C])
        Whi = sb("Whi", [P, C], F32R)
        Wlo = sb("Wlo", [P, C], F32R)
        half_p = sb("half_p", [P, TT])
        half_n = sb("half_n", [P, GQ])
        MR = sb("MR", [P, 2, G])
        flag = sb("flag", [1, 1], I32)

        l0 = ExitStack()
        Wt = sb("Wt", [P, WS, Q, CJ, C], c=l0)
        Z = sb("Z", [P, ZS, CJ, C], c=l0)
        E = sb("E", [P, 2, CJ, C], c=l0)
        ET = sb("ET", [P, 2, CJ, C], c=l0)
        LP = sb("LP", [P, 2, CJ, C], c=l0)
        LS = sb("LS", [P, 2, CJ, C], c=l0)
        nmx = sb("nmx", [P, MS, CJ], c=l0)
        st = sb("st", [P, SP1, G, 6], c=l0)
        dev = sb("dev", [P, G, SP1, 2], c=l0)
        gsum = sb("gsum", [P, G], c=l0)
        gvar = sb("gvar", [P, G], c=l0)
        gown = sb("gown", [P, GQ], c=l0)
        gpow = sb("gpow", [P, GQ], c=l0)
        spread = sb("spread", [P, G], c=l0)
        col = sb("col", [P, 1], c=l0)
        mcol = sb("mcol", [P, 2], c=l0)
        ones = sb("ones", [P, B], c=l0)
        same_image = sb("same_image", [P, P], c=l0)
        adj_sb = sb("adj_sb", [P, C], c=l0)
        aff_sb = sb("aff_sb", [P, C], c=l0)
        l0.close()
        l1 = ExitStack()
        tok = sb("tok", [P, TT, C], c=l1)
        res = sb("res", [P, HT, C], c=l1)
        nTh = sb("nTh", [P, 2, NPOS], F32R, l1)
        nTl = sb("nTl", [P, 2, NPOS], F32R, l1)
        uTh = sb("uTh", [P, 3, HW], F32R, l1)
        uTl = sb("uTl", [P, 3, HW], F32R, l1)
        hh = sb("hh", [P, 2, TT, C], F32R, l1)
        hl = sb("hl", [P, 2, TT, C], F32R, l1)
        Ph = sb("Ph", [P, PB, HW], F32R, l1)
        Pl = sb("Pl", [P, PB, HW], F32R, l1)
        nT = sb("nT", [P, NPOS], c=l1)
        hf = sb("hf", [P, HT, C], c=l1)
        OT = sb("OT", [P, HW], c=l1)
        Y = sb("Y", [P, 2, HT, C], c=l1)
        HF = hf[:, :, :].rearrange("p t c -> p (t c)")
        Y_tok = Y[:, :, :, :].rearrange("p e t c -> p (e t) c")
        YQ = OT[:, :].rearrange("p (t c) -> p t c", c=C)
        mrb = sb("mrb", [P, 2, G], c=l1)
        n2 = sb("n2", [P, TT], c=l1)
        nrm = sb("nrm", [P, 2, TT], c=l1)
        junk = sb("junk", [P, 2, C], c=l1)
        rn = sb("rn", [P, TT], c=l1)
        lastc = sb("lastc", [P, HT], c=l1)
        rs = sb("rs", [P, HT], c=l1)
        vs = sb("vs", [P, HT], c=l1)
        fac = sb("fac", [P, HT], c=l1)
        den = sb("den", [P, HT], c=l1)
        gmx = sb("gmx", [P, 1], c=l1)
        gnm = sb("gnm", [P, 1], c=l1)
        l1.close()

        PS = ctx.enter_context(nc.psum_tensor("PS", [P, 8, 512], F32))
        TP = [PS[:, i, :] for i in (0, 1)]
        PP = [PS[:, i, :] for i in (2, 3)]
        SS = [PS[:, i, :] for i in (4, 5)]
        MISC = PS[:, 6, :]
        SL = [PS[:, i, :] for i in range(SB)]
        OO = [PS[:, i, :] for i in (4, 5)]
        WB = [PS[:, i, :] for i in (6, 7)]

        params_loaded = sem("params_loaded")
        consts_made = sem("consts_made")
        adj_split = sem("adj_split")
        aff_transposed = sem("aff_transposed")
        value_weights_steps = sem("value_weights_steps")
        gram_ready = sem("gram_ready")
        gram_squared = sem("gram_squared")
        bound_summed = sem("bound_summed")
        flag_ready = sem("flag_ready")
        image_loaded = [sem(f"s_load{i}") for i in range(SP0)]
        weights_loaded = [sem(f"s_weights{i}") for i in range(WS)]
        piece_stats_taken = sem("piece_stats_taken")
        stat_steps = sem("stat_steps")
        stat_sums = sem("stat_sums")
        stat_powers = sem("stat_powers")
        chunk_centred = sem("chunk_centred")
        chunk_normalised = sem("chunk_normalised")
        maxima_ready = sem("maxima_ready")
        exp_ready = sem("exp_ready")
        exp_transposed = sem("exp_transposed")
        expT_ready = sem("expT_ready")
        products_ready = sem("products_ready")
        logs_ready = sem("logs_ready")
        chunk_output = sem("chunk_output")
        chunk_added = sem("chunk_added")
        chunk_added_b = sem("chunk_added_b")
        stats_loaded = sem("stats_loaded")
        tokens_loaded = sem("tokens_loaded")
        tokens_free = sem("tokens_free")
        residual_loaded = sem("residual_loaded")
        half_stored = [sem(f"half_stored{i}") for i in (0, 1)]
        tokens_centred = sem("tokens_centred")
        tokens_normed = sem("tokens_normed")
        norm_squared = sem("norm_squared")
        norm_ready = sem("norm_ready")
        norm_guarded = sem("norm_guarded")
        inverse_norm_ready = sem("inverse_norm_ready")
        tokens_unit = sem("tokens_unit")
        tokens_transposed = sem("tokens_transposed")
        nTh_ready = sem("nTh_ready")
        nT_ready = sem("nT_ready")
        nTl_ready = sem("nTl_ready")
        queries_made = sem("queries_made")
        uTh_ready = sem("uTh_ready")
        uTl_ready = sem("uTl_ready")
        values_made = sem("values_made")
        hf_ready = sem("hf_ready")
        hh_ready = sem("hh_ready")
        hl_ready = sem("hl_ready")
        logits_ready = sem("logits_ready")
        weights_ready = sem("weights_ready")
        weights_upper = sem("weights_upper")
        weights_split = sem("weights_split")
        attended = sem("attended")
        output_taken = sem("output_taken")
        rows_made = sem("rows_made")
        rows_taken = sem("rows_taken")
        others_summed = sem("others_summed")
        sums_taken = sem("sums_taken")
        last_channel_set = sem("last_channel_set")
        rows_squared = sem("rows_squared")
        variance_steps = sem("variance_steps")
        inverse_sd_ready = sem("inverse_sd_ready")
        factor_ready = sem("factor_ready")
        rows_scaled = sem("rows_scaled")
        beta_added = sem("beta_added")
        relu_done = sem("relu_done")
        half_done = sem("half_done")
        tile_logits = sem("tile_logits")
        tile_maxima = sem("tile_maxima")
        tile_shift = sem("tile_shift")
        tile_exp = sem("tile_exp")
        tile_transposed = sem("tile_transposed")
        tile_copied = sem("tile_copied")
        tile_attended = sem("tile_attended")

        NST = 10
        NV = 5
        NCONST = 5 + 1 + 2 * Q - 1
        block = ctx.enter_context(nc.Block())
        out_v = out.rearrange("b (p t) c -> b p t c", t=TT)

        @block.sync
        def _(sp):
            sp.dma_start(adj_sb[:, :], adj_w).then_inc(params_loaded, 16)
            sp.dma_start(aff_sb[:, :], aff_w).then_inc(params_loaded, 16)
            for t, v in ((b1, aff_b), (gB, ln_g), (lbB, ln_b)):
                sp.dma_start(t[:, :], v.rearrange("(o c) -> o c", o=1).broadcast_to([P, C])).then_inc(params_loaded, 16)
            xj = J // SP0
            for i in range(SP0):
                sp.dma_start(X[:, i * xj:(i + 1) * xj, :], x[:, i * xj * C:(i + 1) * xj * C]
                             .rearrange("p (j c) -> p j c", c=C)).then_inc(image_loaded[i], 16)

            def load_weights(ch, slot, nth, wait):
                if wait:
                    sp.wait_ge(products_ready, nth)
                sp.dma_start(Wt[:, slot, :, :, :], acc[ch, :, :].rearrange(
                    "k (q i s) -> k q i s", q=Q, i=CJ)).then_inc(weights_loaded[slot], 16)

            for ch in range(WS):
                load_weights(ch, ch, 0, False)
            with sp.Fori(1, NCH // WS) as r:
                for slot in range(WS):
                    load_weights(r * WS + slot, slot, r * WS + slot - WS + 1, True)

            def gather(b, to=tok):
                for q in range(Q):
                    r = q * B + b
                    sp.dma_start(to[q * B:(q + 1) * B, :, :],
                                 X[r:r + 1, :, :].rearrange("o (p t) c -> o p (t c)", t=TT)).then_inc(tokens_loaded, 16)

            def gather_stats(b):
                if b:
                    sp.wait_ge(tokens_normed, b)
                sp.dma_start(mrb[:, :, :], MR[b:b + 1, :, :].unsqueeze(1).broadcast_to([1, P, 2, G]))\
                    .then_inc(stats_loaded, 16)

            def gather_residual(b, e):
                if 2 * b + e:
                    sp.wait_ge(half_done, 2 * b + e)
                for q in range(Q):
                    r = q * B + b
                    sp.dma_start(res[q * B:(q + 1) * B, :, :],
                                 X[r:r + 1, :, :].rearrange("o (p e t) c -> o p e (t c)", e=2, t=HT)[:, :, e, :])\
                        .then_inc(residual_loaded, 16)

            def store(b, e):
                sp.wait_ge(half_done, 2 * b + e + 1)
                sp.dma_start(out_v[b, :, e * HT:(e + 1) * HT, :], Y[:, e, :, :]).then_inc(half_stored[e], 16)

            sp.wait_ge(chunk_added, NCH)
            sp.wait_ge(chunk_added_b, NCH)
            gather(0)
            sp.wait_ge(stat_steps, 2 * NST)
            gather_stats(0)
            sp.wait_ge(flag_ready, 1)
            bounded = sp.value_load(flag[0:1, 0:1], min_val=0, max_val=1)
            with sp.If(bounded == 1):
                sp.wait_ge(tokens_centred, 1)
                gather(1, Y_tok)
                gather_stats(1)
                gather_residual(0, 0)
                for b in range(B):
                    if b + 2 < B:
                        gather_stats(b + 2)
                        sp.wait_ge(tokens_transposed, 2 * (b + 2))
                        gather(b + 2)
                    if b:
                        store(b - 1, 0)
                        gather_residual(b - 1, 1)
                        store(b - 1, 1)
                        gather_residual(b, 0)
                store(B - 1, 0)
                gather_residual(B - 1, 1)
                store(B - 1, 1)
            with sp.Else():
                gather_residual(0, 0)
                for b in range(B):
                    store(b, 0)
                    gather_residual(b, 1)
                    store(b, 1)
                    if b + 1 < B:
                        sp.wait_ge(tokens_free, b + 1)
                        gather(b + 1)
                        gather_stats(b + 1)
                        gather_residual(b + 1, 0)
            sp.wait_ge(half_stored[0], 16 * B)
            sp.wait_ge(half_stored[1], 16 * B)

        @block.gpsimd
        def _(pool):
            n = 0
            for t, v in ((ident, 0.0), (same_image, 0.0), (ones, 1.0), (half_p, 0.5), (half_n, -0.5)):
                pool.memset(t[:, :], v).then_inc(consts_made, 1)
                n += 1
            for t, d in [(ident, 0)] + [(same_image, k * B) for k in range(1 - Q, Q)]:
                pool.wait_ge(consts_made, n)
                pool.affine_select(out=t[:, :], in_=t[:, :], compare_op=ALU.not_equal, fill=1.0, base=-d,
                                   pattern=[[-1, P]], channel_multiplier=1).then_inc(consts_made, 1)
                n += 1
            assert n == NCONST

            def inverse_deviation(turn):
                pool.wait_ge(stat_steps, NST * turn + NST - 2)
                pool.tensor_tensor(gpow[:, :], gown[:, :], half_n[:, :], ALU.pow).then_inc(stat_powers, 1)

            def normalise(c, u, first):
                xc = X[:, bass.ds(c * CJ, CJ), :].rearrange("p j (g k) -> p j g k", k=GC)
                z = Z[:, u % ZS, :, :].rearrange("p j (g k) -> p j g k", k=GC)
                if not first:
                    pool.wait_ge(exp_ready, c - ZS + 1)
                pool.tensor_tensor(z, MR[:, 0, :].unsqueeze(1).unsqueeze(3).broadcast_to([P, CJ, G, GC]), xc,
                                   ALU.subtract).then_inc(chunk_centred, 1)
                pool.wait_ge(chunk_centred, c + 1)
                pool.tensor_tensor(z, z, MR[:, 1, :].unsqueeze(1).unsqueeze(3).broadcast_to([P, CJ, G, GC]),
                                   ALU.mult).then_inc(chunk_normalised, 1)

            def add_output(c, u):
                xc = X[:, bass.ds(c * CJ + HCJ, CJ - HCJ), :]
                pool.wait_ge(chunk_output, c + 1)
                pool.tensor_tensor(xc, LP[:, u % 2, HCJ:CJ, :], xc, ALU.add).then_inc(chunk_added_b, 1)

            inverse_deviation(0)
            pool.wait_ge(stat_steps, NST)
            for c in range(2 * ZS):
                normalise(c, c, c < ZS)
                if c >= BEHIND:
                    add_output(c - BEHIND, c - BEHIND)
            with pool.Fori(2, NCH // ZS) as i:
                for u in range(ZS):
                    normalise(i * ZS + u, u, False)
                    add_output(i * ZS + (u - BEHIND), u - BEHIND)
            for c in range(NCH - BEHIND, NCH):
                add_output(c, c)
            inverse_deviation(1)

            def by_group(t):
                return t.rearrange("p t (g k) -> p t g k", k=GC)

            def centre(b, t=tok[:, :, :]):
                t = by_group(t)
                pool.wait_ge(stats_loaded, b * 16 + 16)
                pool.wait_ge(tokens_loaded, b * (16 * Q) + 16 * Q)
                pool.tensor_tensor(t, t, mrb[:, 0, :].unsqueeze(1).unsqueeze(3).broadcast_to([P, TT, G, GC]),
                                   ALU.subtract).then_inc(tokens_centred, 1)

            def group_norm(b, t=tok[:, :, :]):
                t = by_group(t)
                pool.wait_ge(tokens_centred, b + 1)
                pool.tensor_tensor(t, t, mrb[:, 1, :].unsqueeze(1).unsqueeze(3).broadcast_to([P, TT, G, GC]),
                                   ALU.mult).then_inc(tokens_normed, 1)

            def root(b, s):
                pool.wait_ge(norm_squared, (b + 1) * TT)
                pool.tensor_tensor(nrm[:, s, :], n2[:, :], half_p[:, :], ALU.pow).then_inc(norm_ready, 1)

            def unit(b, t=tok[:, :, :], freed=None):
                pool.wait_ge(inverse_norm_ready, b + 1)
                if freed is not None:
                    pool.wait_ge(*freed)
                pool.tensor_tensor(tok[:, :, :], t, rn[:, :].unsqueeze(2).broadcast_to([P, TT, C]),
                                   ALU.mult).then_inc(tokens_unit, 1)

            def values_lower(b, s, e):
                half = slice(e * HT, (e + 1) * HT)
                pool.wait_ge(hh_ready, b * 2 + (e + 1))
                pool.tensor_tensor(hl[:, s, half, :], hf[:, :, :], hh[:, s, half, :].bitcast(F32),
                                   ALU.subtract).then_inc(hl_ready, 1)

            def squares(b, e):
                pool.wait_ge(last_channel_set, b * 2 + (e + 1))
                pool.tensor_tensor(YQ[:, :, :], Y[:, e, :, :], Y[:, e, :, :], ALU.mult).then_inc(rows_squared, 1)

            def inverse_sd(b, e):
                pool.wait_ge(variance_steps, (b * 2 + (e + 1)) * NV)
                pool.tensor_tensor(vs[:, :], vs[:, :], half_n[:, 0:HT], ALU.pow).then_inc(inverse_sd_ready, 1)

            def add_beta(b, e):
                pool.wait_ge(rows_scaled, b * 2 + (e + 1))
                pool.tensor_tensor(Y[:, e, :, :], Y[:, e, :, :], lbB[:, :].unsqueeze(1).broadcast_to([P, HT, C]),
                                   ALU.add).then_inc(beta_added, 1)

            def add_residual(b, e):
                pool.wait_ge(relu_done, b * 2 + (e + 1))
                pool.wait_ge(residual_loaded, (b * 2 + (e + 1)) * (16 * Q))
                pool.tensor_tensor(Y[:, e, :, :], Y[:, e, :, :], res[:, :, :], ALU.add).then_inc(half_done, 1)

            def image(b, s, first=False, second=False, last=False, late=False):
                if first:
                    unit(1, Y_tok, (tokens_transposed, 2))
                elif not last:
                    unit(b + 1)
                if not (first or second):
                    add_residual(b - 2, 1)
                if not first:
                    squares(b - 1, 0)
                    values_lower(b, s, 1)
                    inverse_sd(b - 1, 0)
                    add_beta(b - 1, 0)
                    add_residual(b - 1, 0)
                    squares(b - 1, 1)
                if not (last or late):
                    centre(b + 2)
                if not (last or late):
                    group_norm(b + 2)
                if not first:
                    inverse_sd(b - 1, 1)
                    add_beta(b - 1, 1)
                if not (last or late):
                    pool.wait_ge(hf_ready, b * 2 + 2)
                    root(b + 2, s)
                if not last:
                    values_lower(b + 1, 1 - s, 0)

            def attention():
                root(0, 0)
                centre(1, Y_tok)
                group_norm(1, Y_tok)
                root(1, 1)
                image(0, 0, first=True)
                image(1, 1, second=True)
                with pool.Fori(1, B // 2 - 1) as i:
                    image(i * 2, 0)
                    image(i * 2 + 1, 1)
                image(B - 2, 0, late=True)
                image(B - 1, 1, last=True)
                add_residual(B - 2, 1)
                squares(B - 1, 0)
                inverse_sd(B - 1, 0)
                add_beta(B - 1, 0)
                add_residual(B - 1, 0)
                inverse_sd(B - 1, 1)

            def general():
                with pool.Fori(0, B) as b:
                    centre(b)
                    group_norm(b)
                    root(b, 0)
                    unit(b)
                    for e in (0, 1):
                        values_lower(b, 0, e)
                    for e in (0, 1):
                        squares(b, e)
                        inverse_sd(b, e)
                        add_beta(b, e)
                        add_residual(b, e)

            pool.wait_ge(flag_ready, 1)
            bounded = pool.value_load(flag[0:1, 0:1], min_val=0, max_val=1)
            with pool.If(bounded == 1):
                attention()
            with pool.Else():
                general()

        @block.scalar
        def _(act):
            act.preload_act_table_set("natural_log_exp_and_others")
            act.wait_ge(gram_ready, 1)
            act.activation(LP[:, 0, 0, :], PP[1][:, 0:C], ACT.Square, accum_out=col[:, :]).then_inc(gram_squared, 1)

            def exps(c, u):
                act.wait_ge(maxima_ready, c + 1)
                for i in range(CJ):
                    last = act.activation(E[:, u % 2, i, :], Z[:, u % ZS, i, :], ACT.Exp,
                                          bias=nmx[:, u % MS, i:i + 1], scale=-1.0)
                last.then_inc(exp_ready, 1)

            def logs(c, u, early=False):
                act.wait_ge(products_ready, c + 1)
                if early:
                    act.wait_ge(gram_squared, 1)
                else:
                    act.wait_ge(chunk_added, c - 1)
                    act.wait_ge(chunk_added_b, c - 1)
                act.activation(LP[:, u % 2, :, :], PP[u % 2].rearrange("p (i c) -> p i c", c=C), ACT.Ln)
                act.activation(LS[:, u % 2, :, :], SS[u % 2].rearrange("p (i c) -> p i c", c=C), ACT.Ln)\
                    .then_inc(logs_ready, 1)

            def step(c, u, first=False, early=False, last=False):
                if not last:
                    if not first:
                        act.wait_ge(exp_transposed, c)
                    exps(c + 1, u + 1)
                act.wait_ge(exp_transposed, c + 1)
                act.activation(ET[:, u % 2, :, :], TP[u % 2].rearrange("p (i c) -> p i c", c=C), ACT.Copy)\
                    .then_inc(expT_ready, 1)
                if not first:
                    logs(c - 1, u - 1, early=early)

            exps(0, 0)
            for c in range(U0):
                step(c, c, first=c == 0, early=c <= 2)
            with act.Fori(1, NCH // U0 - 1) as i:
                for u in range(U0):
                    step(i * U0 + u, U0 + u)
            for c in range(NCH - U0, NCH):
                step(c, c, last=c == NCH - 1)
            logs(NCH - 1, NCH - 1)

            def token_squares(b, tiles, first=False, of=tok):
                act.wait_ge(tokens_normed, b + 1)
                if not first:
                    act.wait_ge(norm_ready, b)
                for t in tiles:
                    if t >= 2 or not first:
                        act.wait_ge(norm_squared, b * TT + (t - 1))
                    act.activation(junk[:, t % 2, :], of[:, t, :], ACT.Square, accum_out=n2[:, t:t + 1])\
                        .then_inc(norm_squared, 1)

            def tokens_T(b, s, e, freed):
                act.wait_ge(tokens_transposed, b * 2 + (e + 1))
                if freed is not None:
                    act.wait_ge(*freed)
                act.activation(nT[:, e * HW:(e + 1) * HW], WB[e], ACT.Copy).then_inc(nT_ready, 1)
                act.activation(nTh[:, s, e * HW:(e + 1) * HW], WB[e], ACT.Copy).then_inc(nTh_ready, 1)

            def queries_T(b, s, e, freed=None):
                act.wait_ge(queries_made, b * 2 + (e + 1))
                if freed is not None:
                    act.wait_ge(*freed)
                act.activation(uTh[:, e * (1 + s), :], WB[e], ACT.Copy).then_inc(uTh_ready, 1)

            def take_output(b, e, made, first=False, to=OT):
                act.wait_ge(*made)
                if not (first or to is HF):
                    act.wait_ge(variance_steps, (b * 2 + e) * NV)
                act.activation(to[:, :], OO[e], ACT.Copy).then_inc(output_taken, 1)

            def take_rows(b, e, first=False):
                act.wait_ge(rows_made, b * 2 + (e + 1))
                if not first:
                    act.wait_ge(half_stored[e], b * 16)
                act.activation(Y[:, e, :, :], WB[e].rearrange("p (t c) -> p t c", c=C), ACT.Copy)\
                    .then_inc(rows_taken, 1)

            def unit_step(b, k, first):
                sl = SL[k % SB]
                act.wait_ge(logits_ready, b * UN + (k + 1))
                if not (first and k < PB):
                    act.wait_ge(attended, b * UN + (k + 1 - SINCE[k]))
                act.activation(Ph[:, SLOT[k], :], sl, ACT.Exp, scale=SHARP).then_inc(weights_upper, 1)
                act.activation(sl, sl, ACT.Exp, scale=SHARP).then_inc(weights_ready, 1)

            def image(b, s, first=False, second=False, last=False, late=False):
                T0 = 5 if first else 3
                for k in range(UN):
                    unit_step(b, k, first)
                    if k == 0 and first:
                        queries_T(0, 0, 1)
                        token_squares(1, range(HT, TT), of=Y_tok)
                    if k == T0 and not last:
                        tokens_T(b + 1, 1 - s, 0, None if first else (logits_ready, b * UN))
                    if k == 4 and not first:
                        take_output(b - 1, 1, (attended, b * UN))
                    if k == 6 and not first:
                        take_rows(b - 1, 1, first=second)
                    if k == 7 and not last:
                        queries_T(b + 1, 1 - s, 0, (logits_ready, b * UN + TT))
                    if k == 9 and not last:
                        tokens_T(b + 1, 1 - s, 1, None)
                    if k == (11 if last else 12):
                        take_output(b, 0, (attended, b * UN + TT), first=first)
                    if k == 12 and not last:
                        queries_T(b + 1, 1 - s, 1)
                    if k == (13 if last else 15):
                        take_rows(b, 0, first=first)
                    if k in (13, 14) and not (last or late):
                        token_squares(b + 2, range(HT) if k == 13 else range(HT, TT))

            def prepare(b):
                for e in (0, 1):
                    tokens_T(b, 0, e, None)
                for e in (0, 1):
                    queries_T(b, 0, e)

            def attention():
                token_squares(0, range(TT), first=True)
                for e in (0, 1):
                    tokens_T(0, 0, e, None)
                queries_T(0, 0, 0)
                token_squares(1, range(HT), of=Y_tok)
                image(0, 0, first=True)
                image(1, 1, second=True)
                with act.Fori(1, B // 2 - 1) as i:
                    image(i * 2, 0)
                    image(i * 2 + 1, 1)
                image(B - 2, 0, late=True)
                image(B - 1, 1, last=True)
                take_output(B - 1, 1, (attended, B * UN), to=HF)
                take_rows(B - 1, 1)

            def general():
                def general_image(b, first):
                    token_squares(b, range(TT), first)
                    prepare(b)
                    act.wait_ge(values_made, b * 2 + 2)
                    for t in range(TT):
                        act.wait_ge(tile_shift, b * TT + (t + 1))
                        if t:
                            act.wait_ge(tile_attended, b * TT + t)
                        act.activation(tok[:, :, :].rearrange("p t c -> p (t c)"),
                                       PS[:, 0:2, :].rearrange("p a c -> p (a c)"), ACT.Exp,
                                       bias=gnm[:, :], scale=SHARP).then_inc(tile_exp, 1)
                        for e in (0, 1):
                            act.wait_ge(tile_transposed, b * (2 * TT) + (2 * t + e + 1))
                            act.activation(nT[:, e * HW:(e + 1) * HW], SL[2 + e], ACT.Copy).then_inc(tile_copied, 1)
                    for e in (0, 1):
                        take_output(b, e, (tile_attended, b * TT + (e + 1) * HT), first=first and e == 0)
                        take_rows(b, e, first=first)

                general_image(0, True)
                with act.Fori(1, B) as b:
                    general_image(b, False)

            act.wait_ge(flag_ready, 1)
            bounded = act.value_load(flag[0:1, 0:1], min_val=0, max_val=1)
            with act.If(bounded == 1):
                attention()
            with act.Else():
                general()

        @block.vector
        def _(dve):
            dve.wait_ge(params_loaded, 16 * 5)
            dve.tensor_copy(Whi[:, :], adj_sb[:, :]).then_inc(adj_split, 1)
            dve.wait_ge(adj_split, 1)
            dve.tensor_tensor(Wlo[:, :], adj_sb[:, :], Whi[:, :].bitcast(F32), ALU.subtract).then_inc(adj_split, 1)
            dve.wait_ge(aff_transposed, 1)
            dve.reduce_sum(mcol[:, 0:1], PP[0][:, 0:C], AX.X).then_inc(value_weights_steps, 1)
            dve.reduce_sum(mcol[:, 1:2], b1[:, :], AX.X).then_inc(value_weights_steps, 1)
            dve.wait_ge(value_weights_steps, 2)
            dve.tensor_scalar(mcol[:, :], mcol[:, :], 1.0 / C, None, ALU.mult).then_inc(value_weights_steps, 1)
            dve.wait_ge(value_weights_steps, 3)
            dve.tensor_scalar(Ac[:, :], PP[0][:, 0:C], mcol[:, 0:1], None, ALU.subtract)\
                .then_inc(value_weights_steps, 1)
            dve.tensor_scalar(b1[:, :], b1[:, :], mcol[:, 1:2], None, ALU.subtract).then_inc(value_weights_steps, 1)
            dve.wait_ge(value_weights_steps, 5)
            dve.memset(Ac[:, C - 1:C], 0.0).then_inc(value_weights_steps, 1)
            dve.memset(b1[:, C - 1:C], 1.0).then_inc(value_weights_steps, 1)
            dve.wait_ge(bound_summed, 1)
            dve.tensor_scalar(flag[0:1, 0:1], PP[1][0:1, C:C + 1], SHARP**4, LIMIT**4, ALU.mult, ALU.is_le)\
                .then_inc(flag_ready, 1)

            def piece_stats(m, pieces, groups):
                for g in groups:
                    last = dve.bn_stats(st[:, m, g, :] if isinstance(m, int) else st[:, bass.ds(m, 1), g, :],
                                        X[:, bass.ds(m * (J // pieces), J // pieces), g * GC:(g + 1) * GC])
                return last

            def statistics(turn, pieces):
                parts = st[:, 0:pieces, :, :].rearrange("p m g (e s) -> p g m e s", s=3)
                n = J // pieces * GC // 2
                d = dev[:, :, 0:pieces, :]
                at = NST * turn
                dve.wait_ge(piece_stats_taken, SP0 + SP1 * turn)
                dve.tensor_reduce(gsum[:, :], parts[:, :, :, :, 1], AX.XY, ALU.add).then_inc(stat_steps, 1)
                dve.wait_ge(stat_sums, 3 * turn + 1)
                dve.tensor_scalar(MR[:, 0, :], MISC[:, 0:G], 1.0 / (2 * pieces * Q), None, ALU.mult)\
                    .then_inc(stat_steps, 1)
                dve.wait_ge(stat_steps, at + 2)
                dve.tensor_tensor(d, parts[:, :, :, :, 1],
                                  MR[:, 0, :].unsqueeze(2).unsqueeze(3).broadcast_to([P, G, pieces, 2]),
                                  ALU.subtract).then_inc(stat_steps, 1)
                dve.wait_ge(stat_steps, at + 3)
                dve.tensor_tensor(d, d, d, ALU.mult).then_inc(stat_steps, 1)
                dve.wait_ge(stat_steps, at + 4)
                dve.tensor_reduce(gvar[:, :], d, AX.XY, ALU.add).then_inc(stat_steps, 1)
                dve.tensor_reduce(gsum[:, :], parts[:, :, :, :, 2], AX.XY, ALU.add).then_inc(stat_steps, 1)
                dve.wait_ge(stat_steps, at + 6)
                dve.scalar_tensor_tensor(out=gsum[:, :], in0=gvar[:, :], scalar=float(n), in1=gsum[:, :],
                                         op0=ALU.mult, op1=ALU.add).then_inc(stat_steps, 1)
                dve.wait_ge(stat_sums, 3 * turn + 2)
                for q in range(Q):
                    rows, own = slice(q * B, (q + 1) * B), slice(G + q * GQ, G + (q + 1) * GQ)
                    last = dve.tensor_scalar(gown[rows, :], MISC[rows, own], 1.0 / (NPOS * GC), GN_EPS,
                                             ALU.mult, ALU.add)
                last.then_inc(stat_steps, 1)
                dve.wait_ge(stat_powers, turn + 1)
                for q in range(Q):
                    rows, own = slice(q * B, (q + 1) * B), slice(q * GQ, (q + 1) * GQ)
                    last = dve.tensor_copy(spread[rows, own], gpow[rows, :])
                last.then_inc(stat_steps, 1)
                dve.wait_ge(stat_sums, 3 * turn + 3)
                dve.tensor_copy(MR[:, 1, :], MISC[:, 2 * G:3 * G]).then_inc(stat_steps, 1)

            dve.memset(spread[:, :], 0.0).then_inc(value_weights_steps, 1)
            dve.wait_ge(value_weights_steps, 8)
            for m in range(SP0):
                dve.wait_ge(image_loaded[m], 16)
                piece_stats(m, SP0, range(G)).then_inc(piece_stats_taken, 1)
            statistics(0, SP0)

            def minima(c, u):
                dve.wait_ge(chunk_normalised, c + 1)
                dve.tensor_reduce(nmx[:, u % MS, :], Z[:, u % ZS, :, :], AX.X, ALU.min).then_inc(maxima_ready, 1)

            def result(c, u):
                dve.wait_ge(logs_ready, c + 1)
                for i in range(CJ):
                    last = dve.scalar_tensor_tensor(out=LP[:, u % 2, i, :], in0=LP[:, u % 2, i, :],
                                                    scalar=nmx[:, u % MS, i:i + 1], in1=LS[:, u % 2, i, :],
                                                    op0=ALU.subtract, op1=ALU.subtract)
                last.then_inc(chunk_output, 1)

            def add_output(c, u):
                dve.wait_ge(chunk_output, c + 1)
                xc = X[:, bass.ds(c * CJ, HCJ), :]
                dve.tensor_tensor(xc, LP[:, u % 2, 0:HCJ, :], xc, ALU.add).then_inc(chunk_added, 1)

            for c in range(AHEAD):
                minima(c, c)

            def chunks(i, first=False, last=False):
                for u in range(U0):
                    if not (last and u + AHEAD >= U0):
                        minima(i * U0 + (u + AHEAD), u + AHEAD)
                    result(i * U0 + u, u)
                    if not first and u >= USKIP:
                        if u == USKIP:
                            dve.wait_ge(chunk_added, i * U0)
                            dve.wait_ge(chunk_added_b, i * U0)
                        share = [(v * G) // (U0 - USKIP) for v in (u - USKIP, u - USKIP + 1)]
                        done = piece_stats(i - 1, SP1, range(*share))
                    add_output(i * U0 + u, u)
                if not first:
                    done.then_inc(piece_stats_taken, 1)

            chunks(0, first=True)
            with dve.Fori(1, NCH // U0 - 1) as i:
                chunks(i)
            chunks(NCH // U0 - 1, last=True)
            dve.wait_ge(chunk_added, NCH)
            dve.wait_ge(chunk_added_b, NCH)
            piece_stats(SP1 - 1, SP1, range(G)).then_inc(piece_stats_taken, 1)
            statistics(1, SP1)

            def inverse_norms(b, s):
                dve.wait_ge(norm_ready, b + 1)
                dve.tensor_scalar(nrm[:, s, :], nrm[:, s, :], NORM_MIN, None, ALU.max).then_inc(norm_guarded, 1)
                dve.wait_ge(norm_guarded, b + 1)
                dve.reciprocal(rn[:, :], nrm[:, s, :]).then_inc(inverse_norm_ready, 1)

            def first_group_norm():
                t = tok[:, :, :].rearrange("p t (g k) -> p t g k", k=GC)
                dve.wait_ge(stats_loaded, 16)
                dve.wait_ge(tokens_loaded, 16 * Q)
                dve.tensor_tensor(t, t, mrb[:, 0, :].unsqueeze(1).unsqueeze(3).broadcast_to([P, TT, G, GC]),
                                  ALU.subtract).then_inc(tokens_centred, 1)
                dve.wait_ge(tokens_centred, 1)
                dve.tensor_tensor(t, t, mrb[:, 1, :].unsqueeze(1).unsqueeze(3).broadcast_to([P, TT, G, GC]),
                                  ALU.mult).then_inc(tokens_normed, 1)

            def first_unit():
                dve.wait_ge(inverse_norm_ready, 1)
                dve.tensor_tensor(tok[:, :, :], tok[:, :, :], rn[:, :].unsqueeze(2).broadcast_to([P, TT, C]),
                                  ALU.mult).then_inc(tokens_unit, 1)

            def tokens_lower(b, s, e):
                dve.wait_ge(nTh_ready, b * 2 + (e + 1))
                dve.tensor_tensor(nTl[:, s, e * HW:(e + 1) * HW], WB[e],
                                  nTh[:, s, e * HW:(e + 1) * HW].bitcast(F32), ALU.subtract).then_inc(nTl_ready, 1)

            def queries_lower(b, s, e):
                dve.wait_ge(uTh_ready, b * 2 + (e + 1))
                dve.tensor_tensor(uTl[:, e * (1 + s), :], WB[e], uTh[:, e * (1 + s), :].bitcast(F32),
                                  ALU.subtract).then_inc(uTl_ready, 1)

            def values(b, s, e, first=False):
                n = b * 2 + (e + 1)
                dve.wait_ge(values_made, n)
                if not first:
                    dve.wait_ge(hl_ready, n - 1)
                for t in range(HT):
                    last = dve.scalar_tensor_tensor(out=hf[:, t, :], in0=WB[e][:, t * C:(t + 1) * C],
                                                    scalar=nrm[:, s, e * HT + t:e * HT + t + 1], in1=b1[:, :],
                                                    op0=ALU.mult, op1=ALU.add)
                last.then_inc(hf_ready, 1)

            def values_upper(b, s, e, freed=None):
                n = b * 2 + (e + 1)
                half = slice(e * HT, (e + 1) * HT)
                if freed is not None:
                    dve.wait_ge(*freed)
                dve.wait_ge(hf_ready, n)
                dve.tensor_copy(hh[:, s, half, :], hf[:, :, :]).then_inc(hh_ready, 1)

            def first_values_lower(e):
                half = slice(e * HT, (e + 1) * HT)
                dve.wait_ge(hh_ready, e + 1)
                dve.tensor_tensor(hl[:, 0, half, :], hf[:, :, :], hh[:, 0, half, :].bitcast(F32),
                                  ALU.subtract).then_inc(hl_ready, 1)

            def release(left):
                dve.wait_ge(*left)
                dve.memset(gmx[:, :], 0.0).then_inc(tokens_free, 1)

            def weights_lower(b, k):
                dve.wait_ge(weights_ready, b * UN + (k + 1))
                dve.tensor_tensor(Pl[:, SLOT[k], :], SL[k % SB], Ph[:, SLOT[k], :].bitcast(F32), ALU.subtract)\
                    .then_inc(weights_split, 1)

            def last_channel(b, e):
                n = b * 2 + (e + 1)
                dve.wait_ge(rows_taken, n)
                dve.tensor_reduce(lastc[:, :], Y[:, e, :, 0:C - 1], AX.X, ALU.add).then_inc(others_summed, 1)
                dve.tensor_copy(den[:, :], Y[:, e, :, C - 1]).then_inc(sums_taken, 1)
                dve.wait_ge(others_summed, n)
                dve.wait_ge(sums_taken, n)
                dve.tensor_scalar(Y[:, e, :, C - 1], lastc[:, :], -1.0, None, ALU.mult).then_inc(last_channel_set, 1)

            def variance(b, e):
                n = b * 2 + (e + 1)
                at = (b * 2 + e) * NV
                dve.reciprocal(rs[:, :], den[:, :]).then_inc(variance_steps, 1)
                dve.wait_ge(rows_squared, n)
                dve.reduce_sum(vs[:, :], YQ[:, :, :], AX.X).then_inc(variance_steps, 1)
                dve.wait_ge(variance_steps, at + 2)
                dve.scalar_tensor_tensor(out=vs[:, :], in0=vs[:, :], scalar=1.0 / C, in1=rs[:, :],
                                         op0=ALU.mult, op1=ALU.mult).then_inc(variance_steps, 1)
                dve.wait_ge(variance_steps, at + 3)
                dve.tensor_tensor(vs[:, :], vs[:, :], rs[:, :], ALU.mult).then_inc(variance_steps, 1)
                dve.wait_ge(variance_steps, at + 4)
                dve.tensor_scalar(vs[:, :], vs[:, :], LN_EPS, None, ALU.add).then_inc(variance_steps, 1)

            def scale_rows(b, e):
                n = b * 2 + (e + 1)
                dve.wait_ge(inverse_sd_ready, n)
                dve.tensor_tensor(fac[:, :], vs[:, :], rs[:, :], ALU.mult).then_inc(factor_ready, 1)
                dve.wait_ge(factor_ready, n)
                for t in range(HT):
                    last = dve.scalar_tensor_tensor(out=Y[:, e, t, :], in0=Y[:, e, t, :], scalar=fac[:, t:t + 1],
                                                    in1=gB[:, :], op0=ALU.mult, op1=ALU.mult)
                last.then_inc(rows_scaled, 1)

            def leaky(b, e):
                dve.wait_ge(beta_added, b * 2 + (e + 1))
                y = Y[:, e, :, :]
                dve.scalar_tensor_tensor(out=y, in0=y, scalar=SLOPE, in1=y, op0=ALU.mult, op1=ALU.max)\
                    .then_inc(relu_done, 1)

            def image(b, s, first=False, last=False, late=False):
                T0 = 5 if first else 3
                for k in range(UN):
                    weights_lower(b, k)
                    if k == 0 and first:
                        queries_lower(0, 0, 1)
                    if k in (1, 2) and first:
                        values(0, 0, k - 1, first=k == 1)
                        values_upper(0, 0, k - 1)
                        first_values_lower(k - 1)
                    if k == 1 and first:
                        inverse_norms(1, 1)
                    if k == 0 and not first:
                        last_channel(b - 1, 0)
                    if k == 0 and not first:
                        values(b, s, 1)
                    if k == 3 and not first:
                        variance(b - 1, 0)
                    if k == 3 and not first:
                        values_upper(b, s, 1)
                    if k == T0 + 1 and not last:
                        tokens_lower(b + 1, 1 - s, 0)
                    if k == 5 and not first:
                        scale_rows(b - 1, 0)
                    if k == 7 and not first:
                        leaky(b - 1, 0)
                    if k == 8 and not first:
                        last_channel(b - 1, 1)
                    if k == 8 and not last:
                        queries_lower(b + 1, 1 - s, 0)
                    if k == 9 and not last:
                        tokens_lower(b + 1, 1 - s, 1)
                    if k == 10 and not first:
                        variance(b - 1, 1)
                    if k == (11 if last else 13) and not first:
                        scale_rows(b - 1, 1)
                    if k == 12 and not last:
                        values(b + 1, 1 - s, 0)
                    if k == 13 and not last:
                        values_upper(b + 1, 1 - s, 0, None if first else (attended, b * UN))
                    if k == 12 and not last:
                        queries_lower(b + 1, 1 - s, 1)
                    if k == 15 and not (last or late):
                        inverse_norms(b + 2, s)
                    if k == 14 and last:
                        last_channel(b, 0)
                    if k == 15 and last:
                        variance(b, 0)
                    if k == (13 if last else 14) and not first:
                        leaky(b - 1, 1)

            def prepare(b, first):
                inverse_norms(b, 0)
                tokens_lower(b, 0, 0)
                tokens_lower(b, 0, 1)
                for e in (0, 1):
                    queries_lower(b, 0, e)
                    values(b, 0, e, first=first and e == 0)
                    values_upper(b, 0, e)

            def finish(b, e):
                last_channel(b, e)
                variance(b, e)
                scale_rows(b, e)
                leaky(b, e)

            def last_half(b, e):
                n = b * 2 + (e + 1)
                y = Y[:, e, :, :]
                last_channel(b, e)
                dve.wait_ge(last_channel_set, n)
                dve.tensor_tensor(YQ[:, :, :], y, y, ALU.mult).then_inc(rows_squared, 1)
                leaky(b, 0)
                variance(b, e)
                scale_rows(b, e)
                dve.wait_ge(rows_scaled, n)
                dve.tensor_tensor(y, y, lbB[:, :].unsqueeze(1).broadcast_to([P, HT, C]), ALU.add)\
                    .then_inc(beta_added, 1)
                leaky(b, e)
                dve.wait_ge(relu_done, n)
                dve.wait_ge(residual_loaded, n * (16 * Q))
                dve.wait_ge(half_done, n - 1)
                dve.tensor_tensor(y, y, res[:, :, :], ALU.add).then_inc(half_done, 1)

            def attention():
                first_group_norm()
                inverse_norms(0, 0)
                first_unit()
                for e in (0, 1):
                    tokens_lower(0, 0, e)
                queries_lower(0, 0, 0)
                image(0, 0, first=True)
                image(1, 1)
                with dve.Fori(1, B // 2 - 1) as i:
                    image(i * 2, 0)
                    image(i * 2 + 1, 1)
                image(B - 2, 0, late=True)
                image(B - 1, 1, last=True)
                scale_rows(B - 1, 0)
                last_half(B - 1, 1)

            def general():
                def general_image(b, first):
                    prepare(b, first)
                    for t in range(TT):
                        n = b * TT + (t + 1)
                        dve.wait_ge(tile_logits, n)
                        dve.reduce_max(gmx[:, :], PS[:, 0:2, :].rearrange("p a c -> p (a c)"), AX.X)\
                            .then_inc(tile_maxima, 1)
                        dve.wait_ge(tile_maxima, n)
                        dve.tensor_scalar(gnm[:, :], gmx[:, :], -SHARP, None, ALU.mult).then_inc(tile_shift, 1)
                    release((tile_attended, b * TT + TT))
                    for e in (0, 1):
                        finish(b, e)

                general_image(0, True)
                with dve.Fori(1, B) as b:
                    general_image(b, False)

            dve.wait_ge(flag_ready, 1)
            bounded = dve.value_load(flag[0:1, 0:1], min_val=0, max_val=1)
            with dve.If(bounded == 1):
                attention()
            with dve.Else():
                general()

        @block.tensor
        def _(pe):
            pe.wait_ge(consts_made, NCONST)
            pe.wait_ge(params_loaded, 16 * 5)
            pe.transpose(PP[0][:, 0:C], aff_sb[:, :], ident[:, :]).then_inc(aff_transposed, 1)
            pe.matmul(PP[1][:, 0:C], adj_sb[:, :], adj_sb[:, :], start=True, stop=True).then_inc(gram_ready, 1)
            pe.wait_ge(gram_squared, 1)
            pe.matmul(PP[1][0:B, C:C + 1], ones[:, :], col[:, :], start=True, stop=True).then_inc(bound_summed, 1)

            def sum_quarters(turn):
                for h, (step, t) in enumerate(((1, gsum), (7, gsum), (9, spread))):
                    pe.wait_ge(stat_steps, NST * turn + step)
                    pe.matmul(MISC[:, h * G:(h + 1) * G], same_image[:, :], t[:, :], start=True, stop=True)\
                        .then_inc(stat_sums, 1)

            sum_quarters(0)

            def transposes(c, u, first=False):
                pe.wait_ge(exp_ready, c + 1)
                if not first:
                    pe.wait_ge(expT_ready, c - 1)
                for i in range(CJ):
                    last = pe.transpose(TP[u % 2][:, i * C:(i + 1) * C], E[:, u % 2, i, :], ident[:, :])
                last.then_inc(exp_transposed, 1)

            def products(c, u, nth, first=False):
                w = Wt[:, u % WS, :, :, :]
                pe.wait_ge(weights_loaded[u % WS], nth)
                if not first:
                    pe.wait_ge(logs_ready, c - 1)
                for q in range(Q):
                    pe.matmul(SS[u % 2][q * B:(q + 1) * B, :], ones[:, :], w[:, q, :, :].rearrange("k i s -> k (i s)"),
                              start=True, stop=True)
                pe.wait_ge(expT_ready, c + 1)
                for i in range(CJ):
                    for q in range(Q):
                        last = pe.matmul(PP[u % 2][q * B:(q + 1) * B, i * C:(i + 1) * C],
                                         ET[:, u % 2, i, q * B:(q + 1) * B], w[:, q, i, :], start=True, stop=True)
                last.then_inc(products_ready, 1)

            def chunks(i, first=False, last=False):
                for u in range(U0):
                    if not (last and u == U0 - 1):
                        transposes(i * U0 + (u + 1), u + 1, first=first and u == 0)
                    products(i * U0 + u, u, i * (U0 // WS * 16) + (u // WS + 1) * 16, first=first and u < 2)

            transposes(0, 0, first=True)
            chunks(0, first=True)
            with pe.Fori(1, NCH // U0 - 1) as i:
                chunks(i)
            chunks(NCH // U0 - 1, last=True)
            sum_quarters(1)

            def three(out_, lh, ll, rh, rl, start=True, stop=True):
                pe.matmul(out_, lh, rh, start=start, stop=False)
                pe.matmul(out_, lh, rl, start=False, stop=False)
                return pe.matmul(out_, ll, rh, start=False, stop=stop)

            def transpose_tokens(b, e, freed):
                pe.wait_ge(tokens_unit, b + 1)
                if freed is not None:
                    pe.wait_ge(*freed)
                for t in range(HT):
                    last = pe.transpose(WB[e][:, t * C:(t + 1) * C], tok[:, e * HT + t, :], ident[:, :])
                last.then_inc(tokens_transposed, 1)

            def queries(b, s, e):
                n = b * 2 + (e + 1)
                pe.wait_ge(nTl_ready, n)
                pe.wait_ge(nT_ready, n)
                h = slice(e * HW, (e + 1) * HW)
                three(WB[e], Whi[:, :], Wlo[:, :], nTh[:, s, h], nTl[:, s, h]).then_inc(queries_made, 1)

            def values(b, e):
                n = b * 2 + (e + 1)
                pe.wait_ge(uTl_ready, n)
                for t in range(HT):
                    k = e * HT + t
                    last = pe.matmul(WB[e][:, t * C:(t + 1) * C], nT[:, k * C:(k + 1) * C], Ac[:, :],
                                     start=True, stop=True)
                last.then_inc(values_made, 1)

            def rows(b, e, freed, of=OT):
                pe.wait_ge(output_taken, b * 2 + (e + 1))
                if freed is not None:
                    pe.wait_ge(*freed)
                for t in range(HT):
                    last = pe.transpose(WB[e][:, t * C:(t + 1) * C], of[:, t * C:(t + 1) * C], ident[:, :])
                last.then_inc(rows_made, 1)

            def logits(b, s, k, first):
                e, m = divmod(k, TT)
                if first and k == 0:
                    pe.wait_ge(uTl_ready, 1)
                if not (first and k < SB):
                    pe.wait_ge(weights_split, b * UN + (k + 1 - SB))
                t, u = slice(m * C, (m + 1) * C), e * (1 + s)
                three(SL[k % SB], nTh[:, s, t], nTl[:, s, t], uTh[:, u, :], uTl[:, u, :]).then_inc(logits_ready, 1)

            def attend(b, s, k, first):
                e, m = divmod(k, TT)
                if m == 0 and not first:
                    pe.wait_ge(output_taken, b * 2 + (e - 1))
                if k == 0:
                    pe.wait_ge(hl_ready, b * 2 + 1)
                if k == HT:
                    pe.wait_ge(hl_ready, b * 2 + 2)
                pe.wait_ge(weights_split, b * UN + (k + 1))
                three(OO[e], hh[:, s, m, :], hl[:, s, m, :], Ph[:, SLOT[k], :], Pl[:, SLOT[k], :],
                      start=m == 0, stop=m == TT - 1).then_inc(attended, 1)

            def image(b, s, first=False, last=False, late=False):
                T0 = 5 if first else 3
                for k in range(UN):
                    logits(b, s, k, first)
                    if k >= LAG:
                        attend(b, s, k - LAG, first)
                    elif not first:
                        attend(b - 1, 1 - s, UN + k - LAG, False)
                    if k == 0 and first:
                        queries(0, 0, 1)
                    if k in (1, 2) and first:
                        values(0, k - 1)
                    if k == 0 and not first:
                        values(b, 1)
                    if k == T0 and not last:
                        transpose_tokens(b + 1, 0, (hf_ready, 1) if first else (rows_taken, b * 2 - 1))
                    if k == 6 and not first:
                        rows(b - 1, 1, (hf_ready, b * 2 + 2))
                    if k == 7 and not last:
                        queries(b + 1, 1 - s, 0)
                    if k == 8 and not last:
                        transpose_tokens(b + 1, 1, (hf_ready, 2) if first else (rows_taken, b * 2))
                    if k == 12 and not last:
                        values(b + 1, 0)
                    if k == 12 and not last:
                        queries(b + 1, 1 - s, 1)
                    if k == (13 if last else 15):
                        rows(b, 0, (rows_taken, b * 2 - 1) if last else (hf_ready, b * 2 + 3))

            def prepare(b, freed):
                for e in (0, 1):
                    transpose_tokens(b, e, freed)
                for e in (0, 1):
                    queries(b, 0, e)
                    values(b, e)

            def attention():
                for e in (0, 1):
                    transpose_tokens(0, e, None)
                queries(0, 0, 0)
                image(0, 0, first=True)
                image(1, 1)
                with pe.Fori(1, B // 2 - 1) as i:
                    image(i * 2, 0)
                    image(i * 2 + 1, 1)
                image(B - 2, 0, late=True)
                image(B - 1, 1, last=True)
                for k in range(UN - LAG, UN):
                    attend(B - 1, 1, k, False)
                rows(B - 1, 1, (rows_taken, 2 * (B - 1)), of=HF)

            def general():
                def general_image(b, first):
                    prepare(b, None if first else (rows_taken, b * 2))
                    pe.wait_ge(hl_ready, b * 2 + 2)
                    for t in range(TT):
                        n = b * TT + t
                        if not (first and t == 0):
                            pe.wait_ge(tile_exp, n)
                        if t == 0:
                            pe.wait_ge(uTl_ready, b * 2 + 2)
                        u, q = t // HT, slice(t % HT * C, (t % HT + 1) * C)
                        for e in (0, 1):
                            h = slice(e * HW, (e + 1) * HW)
                            last = three(SL[e], uTh[:, u, q], uTl[:, u, q], nTh[:, 0, h], nTl[:, 0, h])
                        last.then_inc(tile_logits, 1)
                        pe.wait_ge(tile_exp, n + 1)
                        for e in (0, 1):
                            if not (first and t == 0):
                                pe.wait_ge(tile_copied, n * 2 + (e - 1))
                            for k in range(HT):
                                last = pe.transpose(SL[2 + e][:, k * C:(k + 1) * C], tok[:, e * HT + k, :],
                                                    ident[:, :])
                            last.then_inc(tile_transposed, 1)
                        pe.wait_ge(tile_copied, n * 2 + 2)
                        e, k = divmod(t, HT)
                        if k == 0 and not first:
                            pe.wait_ge(output_taken, b * 2 + (e - 1))
                        o = OO[e][:, k * C:(k + 1) * C]
                        for m in range(TT):
                            pt = nT[:, m * C:(m + 1) * C]
                            pe.matmul(o, hh[:, 0, m, :].bitcast(F32), pt, start=m == 0, stop=False)
                            last = pe.matmul(o, hl[:, 0, m, :].bitcast(F32), pt, start=False, stop=m == TT - 1)
                        last.then_inc(tile_attended, 1)
                    for e in (0, 1):
                        rows(b, e, (hf_ready, b * 2 + 2))

                general_image(0, True)
                with pe.Fori(1, B) as b:
                    general_image(b, False)

            pe.wait_ge(flag_ready, 1)
            bounded = pe.value_load(flag[0:1, 0:1], min_val=0, max_val=1)
            with pe.If(bounded == 1):
                attention()
            with pe.Else():
                general()


def kernel(x, L0_conv_accumulators, L1_conv_global_feat, L1_conv_pos, L1_conv_adj_w, L1_conv_affine_w,
           L1_conv_affine_b, L1_conv_ln_g, L1_conv_ln_b):
    import concourse.bacc as bacc
    from concourse.bass_utils import run_bass_kernel_spmd

    arrays = {
        "x": np.asarray(x).reshape(B, Q, J * C).transpose(1, 0, 2).reshape(P, J * C),
        "acc": np.asarray(L0_conv_accumulators).reshape(Q, NCH, CJ, C, C).transpose(1, 3, 0, 2, 4)
        .reshape(NCH, C, Q * CJ * C),
        "adj_w": np.asarray(L1_conv_adj_w),
        "aff_w": np.asarray(L1_conv_affine_w),
        "aff_b": np.asarray(L1_conv_affine_b),
        "ln_g": np.asarray(L1_conv_ln_g),
        "ln_b": np.asarray(L1_conv_ln_b),
    }
    arrays = {k: np.ascontiguousarray(v) for k, v in arrays.items()}
    nc = bacc.Bacc("TRN2", target_bir_lowering=False, num_devices=1)
    ins = [nc.dram_tensor(k, v.shape, F32, kind="ExternalInput").ap() for k, v in arrays.items()]
    out = nc.dram_tensor("out", (B, NPOS, C), F32, kind="ExternalOutput").ap()
    build(nc, *ins, out)
    r = run_bass_kernel_spmd(nc, [arrays], core_ids=[0])
    return r.results[0]["out"].reshape(B, 32, 32, C)
```
